# Optimizing a Trainium2 kernel written in Bass

```python
import numpy as np
import jax
import jax.numpy as jnp

def _softmax(x, axis=-1):
    return jax.nn.softmax(x, axis=axis)

def _gelu(x):
    return jax.nn.gelu(x, approximate=True)

def _silu(x):
    return jax.nn.silu(x)

def _sigmoid(x):
    return jax.nn.sigmoid(x)

def _layernorm(x, axis=-1, eps=1e-05):
    m = jnp.mean(x, axis=axis, keepdims=True)
    v = jnp.var(x, axis=axis, keepdims=True)
    return (x - m) / jnp.sqrt(v + eps)

def _scatter_add(tgt, idx, src, axis=0):
    return tgt.at[idx].add(src)

def _segment_sum(src, seg, n):
    return jax.ops.segment_sum(src, seg, n)
kernel_name = 'mk_hybrid_d1_jaxref_r8_5f1b7d'

def setup_inputs(seed: int=0):
    np.random.seed(seed)
    _w = jnp.asarray

    def _L0_attn_a_setup():
        import jax, jax.numpy as jnp
        import numpy as np
        EMBED_DIM = 128
        NUM_HEADS = 16
        HEAD_DIM = EMBED_DIM // NUM_HEADS
        LN_EPS = 1e-05
        key = jax.random.key(seed)
        ks = jax.random.split(key, 7)
        B, L, D = (4, 512, EMBED_DIM)
        s_in = 1.0 / np.sqrt(D)
        return {'x': jax.random.normal(ks[0], (B, L, D), dtype=jnp.float32), 'w_qkv': jax.random.normal(ks[1], (D, 3 * D), dtype=jnp.float32) * s_in, 'b_qkv': jnp.zeros((3 * D,), dtype=jnp.float32), 'w_out': jax.random.normal(ks[2], (D, D), dtype=jnp.float32) * s_in, 'b_out': jnp.zeros((D,), dtype=jnp.float32), 'ln_g': jnp.ones((D,), dtype=jnp.float32), 'ln_b': jnp.zeros((D,), dtype=jnp.float32)}
    _L0_attn_a_in = _L0_attn_a_setup()

    def _L0_attn_b_setup():
        import jax, jax.numpy as jnp
        import numpy as np
        DIM = 128
        NUM_HEADS = 16
        DIM_HEAD = DIM // NUM_HEADS

        def _softmax(logits, axis=-1):
            logits = logits - jnp.max(logits, axis=axis, keepdims=True)
            e = jnp.exp(logits)
            return e / jnp.sum(e, axis=axis, keepdims=True)
        key = jax.random.key(seed)
        kx, kq, kk, kv, ko = jax.random.split(key, 5)
        s = 1.0 / np.sqrt(DIM)
        return {'x': jax.random.normal(kx, (4, 256, DIM), dtype=jnp.float32), 'Wq': jax.random.uniform(kq, (DIM, DIM), jnp.float32, -s, s), 'Wk': jax.random.uniform(kk, (DIM, DIM), jnp.float32, -s, s), 'Wv': jax.random.uniform(kv, (DIM, DIM), jnp.float32, -s, s), 'Wo': jax.random.uniform(ko, (DIM, DIM), jnp.float32, -s, s)}
    _L0_attn_b_in = _L0_attn_b_setup()

    def _L0_ffn_setup():
        import jax, jax.numpy as jnp
        import numpy as np
        E = 8
        TOP_K = 2
        H = 128
        F = 512
        LN_EPS = 1e-12
        key = jax.random.key(seed)
        ks = jax.random.split(key, 9)
        s = lambda k, shape, scale: jax.random.normal(k, shape, dtype=jnp.float32) * scale
        return {'hidden_states': s(ks[0], (4, 256, H), 1.0), 'Wr': s(ks[1], (E, H), 0.02), 'br': jnp.zeros((E,), jnp.float32), 'W1': s(ks[2], (E, F, H), 0.02), 'b1': jnp.zeros((E, F), jnp.float32), 'W2': s(ks[3], (E, H, F), 0.02), 'b2': jnp.zeros((E, H), jnp.float32), 'ln_w': jnp.ones((H,), jnp.float32), 'ln_b': jnp.zeros((H,), jnp.float32)}
    _L0_ffn_in = _L0_ffn_setup()
    _d = {'L0_attn_a_x': _L0_attn_a_in['x'], 'L0_attn_a_w_qkv': _L0_attn_a_in['w_qkv'], 'L0_attn_a_b_qkv': _L0_attn_a_in['b_qkv'], 'L0_attn_a_w_out': _L0_attn_a_in['w_out'], 'L0_attn_a_b_out': _L0_attn_a_in['b_out'], 'L0_attn_a_ln_g': _L0_attn_a_in['ln_g'], 'L0_attn_a_ln_b': _L0_attn_a_in['ln_b'], 'L0_attn_b_Wq': _L0_attn_b_in['Wq'], 'L0_attn_b_Wk': _L0_attn_b_in['Wk'], 'L0_attn_b_Wv': _L0_attn_b_in['Wv'], 'L0_attn_b_Wo': _L0_attn_b_in['Wo'], 'L0_ffn_Wr': _L0_ffn_in['Wr'], 'L0_ffn_br': _L0_ffn_in['br'], 'L0_ffn_W1': _L0_ffn_in['W1'], 'L0_ffn_b1': _L0_ffn_in['b1'], 'L0_ffn_W2': _L0_ffn_in['W2'], 'L0_ffn_b2': _L0_ffn_in['b2'], 'L0_ffn_ln_w': _L0_ffn_in['ln_w'], 'L0_ffn_ln_b': _L0_ffn_in['ln_b']}
    _x0 = _d['L0_attn_a_x']
    _d['L0_attn_a_x'] = jax.random.normal(jax.random.fold_in(jax.random.key(seed), 1), (8, 512, 128), dtype=_x0.dtype)
    del _x0
    return _d

def reference(L0_attn_a_x, L0_attn_a_w_qkv, L0_attn_a_b_qkv, L0_attn_a_w_out, L0_attn_a_b_out, L0_attn_a_ln_g, L0_attn_a_ln_b, L0_attn_b_Wq, L0_attn_b_Wk, L0_attn_b_Wv, L0_attn_b_Wo, L0_ffn_Wr, L0_ffn_br, L0_ffn_W1, L0_ffn_b1, L0_ffn_W2, L0_ffn_b2, L0_ffn_ln_w, L0_ffn_ln_b):

    def _L0_attn_a_ref(x, w_qkv, b_qkv, w_out, b_out, ln_g, ln_b):
        import jax, jax.numpy as jnp
        import numpy as np
        EMBED_DIM = 128
        NUM_HEADS = 16
        HEAD_DIM = EMBED_DIM // NUM_HEADS
        LN_EPS = 1e-05
        B, L, D = x.shape
        H, hd = (NUM_HEADS, HEAD_DIM)
        residual = x
        mu = jnp.mean(x, axis=-1, keepdims=True)
        var = jnp.mean(jnp.square(x - mu), axis=-1, keepdims=True)
        xn = (x - mu) * jax.lax.rsqrt(var + LN_EPS) * ln_g + ln_b
        qkv = xn @ w_qkv + b_qkv
        q, k, v = jnp.split(qkv, 3, axis=-1)
        q = q.reshape(B, L, H, hd)
        k = k.reshape(B, L, H, hd)
        v = v.reshape(B, L, H, hd)
        kt_v = jnp.einsum('blhd,blhe->bhde', k, v)
        s = jax.nn.softmax(kt_v, axis=-1)
        out = jnp.einsum('blhd,bhde->blhe', q, s).reshape(B, L, D)
        out = out @ w_out + b_out
        return out + residual

    def _L0_attn_b_ref(x, Wq, Wk, Wv, Wo):
        import jax, jax.numpy as jnp
        import numpy as np
        DIM = 128
        NUM_HEADS = 16
        DIM_HEAD = DIM // NUM_HEADS

        def _softmax(logits, axis=-1):
            logits = logits - jnp.max(logits, axis=axis, keepdims=True)
            e = jnp.exp(logits)
            return e / jnp.sum(e, axis=axis, keepdims=True)
        B, T, D = x.shape
        H, Dh = (NUM_HEADS, DIM_HEAD)
        q = (x @ Wq.T).reshape(B, T, H, Dh).transpose(0, 2, 1, 3)
        k = (x @ Wk.T).reshape(B, T, H, Dh).transpose(0, 2, 1, 3)
        v = (x @ Wv.T).reshape(B, T, H, Dh).transpose(0, 2, 1, 3)
        scale = Dh ** (-0.5)
        logits = jnp.einsum('bhqd,bhkd->bhqk', q, k) * scale
        causal_mask = jnp.triu(jnp.ones((T, T), dtype=bool), k=1)
        neg = -jnp.finfo(logits.dtype).max
        logits = jnp.where(causal_mask, neg, logits)
        attn = _softmax(logits, axis=-1)
        out = jnp.einsum('bhqk,bhkd->bhqd', attn, v)
        out = out.transpose(0, 2, 1, 3).reshape(B, T, D)
        return out @ Wo.T

    def _L0_ffn_ref(hidden_states, Wr, br, W1, b1, W2, b2, ln_w, ln_b):
        import jax, jax.numpy as jnp
        import numpy as np
        E = 8
        TOP_K = 2
        H = 128
        F = 512
        LN_EPS = 1e-12
        bsz, seqlen, h = hidden_states.shape
        x = hidden_states.reshape(-1, h)
        logits = x @ Wr.T + br
        topk_vals, topk_idx = jax.lax.top_k(logits, TOP_K)
        topk_w = jax.nn.softmax(topk_vals, axis=-1)
        out = jnp.zeros_like(x)
        for e in range(E):
            cw = jnp.sum(topk_w * (topk_idx == e), axis=-1)
            y = jax.nn.gelu(x @ W1[e].T + b1[e], approximate=False) @ W2[e].T + b2[e]
            out = out + cw[:, None] * y
        z = out + x
        mu = jnp.mean(z, axis=-1, keepdims=True)
        var = jnp.mean(jnp.square(z - mu), axis=-1, keepdims=True)
        z = (z - mu) * jax.lax.rsqrt(var + LN_EPS) * ln_w + ln_b
        return z.reshape(bsz, seqlen, h)
    x = L0_attn_a_x
    x = x + _L0_attn_a_ref(_layernorm(x, axis=-1), L0_attn_a_w_qkv, L0_attn_a_b_qkv, L0_attn_a_w_out, L0_attn_a_b_out, L0_attn_a_ln_g, L0_attn_a_ln_b)
    x = x + _L0_ffn_ref(_layernorm(x, axis=-1), L0_ffn_Wr, L0_ffn_br, L0_ffn_W1, L0_ffn_b1, L0_ffn_W2, L0_ffn_b2, L0_ffn_ln_w, L0_ffn_ln_b)
    x = x + _L0_attn_b_ref(_layernorm(x, axis=-1), L0_attn_b_Wq, L0_attn_b_Wk, L0_attn_b_Wv, L0_attn_b_Wo)
    x = x + _L0_ffn_ref(_layernorm(x, axis=-1), L0_ffn_Wr, L0_ffn_br, L0_ffn_W1, L0_ffn_b1, L0_ffn_W2, L0_ffn_b2, L0_ffn_ln_w, L0_ffn_ln_b)
    return x

_drawn_inputs = setup_inputs


def setup_inputs(seed=0):
    import zlib

    import numpy as np

    out = dict(_drawn_inputs(seed))
    spreads = {'L0_attn_a_b_qkv': (0.0, 0.1),
     'L0_attn_a_b_out': (0.0, 0.1),
     'L0_attn_a_ln_g': (1.0, 0.2),
     'L0_attn_a_ln_b': (0.0, 0.1),
     'L0_ffn_br': (0.0, 0.1),
     'L0_ffn_b1': (0.0, 0.8),
     'L0_ffn_b2': (0.0, 0.1),
     'L0_ffn_ln_w': (1.0, 0.2),
     'L0_ffn_ln_b': (0.0, 0.1)}
    factors = {'L0_attn_b_Wq': 8.0,
     'L0_attn_b_Wk': 8.0,
     'L0_attn_b_Wv': 3.726,
     'L0_attn_b_Wo': 3.642,
     'L0_ffn_W1': 2.673}
    for name, (base, spread) in spreads.items():
        noise = np.random.default_rng([zlib.crc32(name.encode()), seed]).standard_normal(out[name].shape)
        drawn = base * np.exp(spread * noise) if base else spread * noise
        out[name] = jnp.asarray(drawn.astype(out[name].dtype))
    for name, factor in factors.items():
        out[name] = (out[name] * factor).astype(out[name].dtype)
    return out
```

```python
from contextlib import ExitStack

import concourse.bass as bass
import concourse.mybir as mybir
from concourse.alu_op_type import AluOpType as ALU

F32 = mybir.dt.float32
F32R = mybir.dt.float32r
BF16 = mybir.dt.bfloat16
U32 = mybir.dt.uint32
ACT = mybir.ActivationFunctionType
AX = mybir.AxisListType

P = 128
B, L, D = 8, 512, 128
T = L // P
NH, HD = 16, 8
HS = 32
NG = NH // 4
E, F = 8, 512
FT = F // P
J = E * FT
RG = 3
RP = 5
PW = 1280
LAG = 6
NEG = -3.0e38
SCALE = float(HD) ** -0.5
K_OFF = [0, 512, 1024, 896]
K_BANK = [(3, 0), (4, 0), (5, 0), (4, 384)]
Q_BANK = [(1, 384), (2, 0), (1, 0), (0, 0)]

PER = {}


def at(name, n, k):
    return PER[name] * n + k


def build(nc, x, out, w):
    ctx = ExitStack()
    with ctx:
        def sb(name, shape, dt=F32):
            return ctx.enter_context(nc.sbuf_tensor(name, shape, dt))

        S = {}

        def sem(name, per):
            S[name] = ctx.enter_context(nc.semaphore(name))
            PER[name] = per

        def wait(eng, name, n, k):
            v = at(name, n, k)
            if not isinstance(v, int) or v > 0:
                eng.wait_ge(S[name], v)

        def settle(eng):
            eng.nop(nofuse=True)

        ident = sb("ident", [P, P])
        head_mask = sb("head_mask", [P, P])
        causal = sb("causal", [P, L])
        ident_b = sb("ident_b", [P, P], BF16)
        later = sb("later", [P, P], BF16)
        expert_id = sb("expert_id", [P, T, 2, E])
        minus_half = sb("minus_half", [P, T])
        base_e = sb("base_e", [P, T])
        low_rows = sb("low_rows", [P, 2])
        max_rows = sb("max_rows", [P, 2])
        pick = sb("pick", [2 * E, E, P], F32R)
        w1h, w1l = sb("w1h", [P, J * P], F32R), sb("w1l", [P, J * P], F32R)
        w2h, w2l = sb("w2h", [P, J * P], F32R), sb("w2l", [P, J * P], F32R)
        b1 = sb("b1", [P, J])
        b2 = sb("b2", [2 * E, D])
        wsh, wsl = sb("wsh", [P, 2, NG * P], F32R), sb("wsl", [P, 2, NG * P], F32R)
        wvh, wvl = sb("wvh", [P, D], F32R), sb("wvl", [P, D], F32R)
        wo = sb("wo", [P, D])
        wqkv = sb("wqkv", [P, 3 * D])
        wout = sb("wout", [P, D])
        wrh, wrl = sb("wrh", [P, E], F32R), sb("wrl", [P, E], F32R)
        bkv = sb("bkv", [P, 2 * D])
        bout = sb("bout", [P, D])
        lnw, lnb = sb("lnw", [P, D]), sb("lnb", [P, D])
        br = sb("br", [P, E])
        cols = sb("cols", [P, 3])

        x0, xa, nrm = sb("x0", [P, T, D]), sb("xa", [P, T, D]), sb("nrm", [P, T, D])
        x1, x2, x3 = sb("x1", [P, T, D]), sb("x2", [P, T, D]), sb("x3", [P, T, D])
        h = [sb("h1", [P, T, D]), sb("h3", [P, T, D])]
        z = sb("z", [P, T, D])
        hh = [sb("hh0", [P, L], F32R), sb("hh1", [P, L], F32R)]
        hl = [sb("hl0", [P, L], F32R), sb("hl1", [P, L], F32R)]
        xnT = sb("xnT", [P, L])
        qT = sb("qT", [P, L])
        kv = sb("kv", [P, T, 2 * D])
        sm = sb("sm", [P, P])
        smx = sb("smx", [P, 4])
        cwT = [sb("cwT0", [2 * E, L], F32R), sb("cwT1", [2 * E, L], F32R)]
        mix = sb("mix", [P, E, L])
        acc = sb("acc", [P, L])
        work = sb("work", [P, RP * PW])
        g32 = [work[:, k * L:(k + 1) * L] for k in range(RG)]
        weighted = [work[:, (RG + k) * L:(RG + k + 1) * L] for k in range(2)]
        parts = sb("parts", [P, 10 * L], F32R)
        gh = [parts[:, k * L:(k + 1) * L] for k in range(RG)]
        gl = [parts[:, (RG + k) * L:(RG + k + 1) * L] for k in range(RG)]
        stack = [[parts[:, (2 * g + s) * L:(2 * g + s + 1) * L] for s in range(2)] for g in range(NG)]
        stack_low = [parts[:, (8 + s) * L:(9 + s) * L] for s in range(2)]
        V = sb("V", [P, T, NH, HS])
        hmax = sb("hmax", [P, NG, 4, T])
        spread = sb("spread", [P, T, P])
        junk = sb("junk", [P, 2, L], BF16)
        oT = sb("oT", [P, L])
        inv = sb("inv", [P, T, 4])
        o = sb("o", [P, T, D])
        LNS = ["la", "lb", "l1", "l2", "l3", "z1", "z2"]
        ln = {k: (sb(f"{k}_st", [P, T, 6]), sb(f"{k}_mv", [P, T, 2]), sb(f"{k}_ve", [P, T]), sb(f"{k}_rs", [P, T]))
              for k in LNS}
        lg = sb("lg", [P, T, E])
        top = sb("top", [P, T, E])
        topi = sb("topi", [P, T, E], U32)
        topf = sb("topf", [P, T, 2])
        gap, ratio, one_more = sb("gap", [P, T]), sb("ratio", [P, T]), sb("one_more", [P, T])
        share = sb("share", [P, T, 2])
        chosen = sb("chosen", [P, T, 2, E])
        cw = sb("cw", [P, T, E])
        cwp = sb("cwp", [P, T, 2 * E])

        bank = [ctx.enter_context(nc.psum_tensor(f"bank{k}", [P, L], F32)) for k in range(8)]
        PV, MISC = bank[6], bank[7]

        LOADS = ["w1", "w2", "b1", "b2a", "b2b", "wk", "wq", "wv", "wo", "wqkv", "wout", "wr", "bkv", "bout",
                 "lnw", "br", "g", "b", "bq"]
        for k in LOADS:
            sem("ld_" + k, 16)
        sem("x_loaded", 16)
        sem("z_stored", 16)
        sem("pool_const", 1)
        sem("dve_const", 1)
        sem("w1_split", 1)
        sem("w2_split", 1)
        for k in LNS:
            sem(k + "_stats", T)
            sem(k + "_moments", T)
            sem(k + "_vareps", 1)
            sem(k + "_rstd", 1)
            sem(k + "_normed", T)
        sem("up_done", J)
        sem("gelu_done", J)
        sem("split_done", J)
        sem("down_done", J)
        sem("weighted_done", E)
        sem("summed", E - 1)
        for s in "12":
            sem(f"z{s}_back", 1)
            sem(f"z{s}_resid", 1)
            sem(f"z{s}_affine", 2)
            sem(f"x{2 * int(s) - 1}_biased", 1)
        for t in "123":
            sem(f"t{t}_turned", 1)
            sem(f"t{t}_high", 1)
            sem(f"t{t}_low", 1)
        for r in "12":
            sem(f"r{r}_logits", 1)
            sem(f"r{r}_pick", 10)
            sem(f"r{r}_ratio", 1)
            sem(f"r{r}_share", 9)
            sem(f"r{r}_turned", 1)
            sem(f"r{r}_cwT", 1)
            sem(f"r{r}_spread", E)
            sem(f"r{r}_mix", E)
        sem("x0_sums", 2)
        sem("xn_turned", 1)
        sem("xn_ready", 1)
        sem("kv_done", 2)
        sem("kv_biased", 2)
        sem("q_done", 1)
        sem("q_biased", 1)
        sem("ktv_done", 1)
        sem("ktv_max", 2)
        sem("ktv_exp", 1)
        sem("ktv_soft", 2)
        sem("lin_mixed", 1)
        sem("lin_copied", 1)
        sem("lin_out", 1)
        sem("x1_done", 1)
        sem("stack_mm", 2 * NG)
        sem("stack_low", 2 * NG)
        sem("stack_done", 2 * NG)
        sem("v_mm", 1)
        sem("v_done", 1)
        sem("logit_mm", 3 * NH)
        sem("max_done", 4 * NH)
        sem("max_spread", 2 * NG)
        sem("max_turned", NG)
        sem("max_in_q", NG)
        sem("pair_mm", 3 * NH)
        sem("exp_done", 3 * NH)
        sem("pv_done", NG)
        sem("pv_copied", NG)
        sem("pv_turned", NG)
        sem("inv_done", NG)
        sem("o_normed", NG)
        sem("o_turned", 1)
        sem("o_copied", 1)
        sem("wo_done", 1)
        sem("x3_done", 1)

        x_tiles = x.rearrange("b (t p) d -> b p t d", p=P)
        out_tiles = out.rearrange("b (t p) d -> b p t d", p=P)

        def every_iteration(eng, body):
            body(0, False, True)
            with eng.Fori(1, B - 1) as i:
                body(i, True, True)
            body(B - 1, True, False)
            body(B, True, False)

        block = ctx.enter_context(nc.Block())

        @block.sync
        def _(sp):
            def load(name, dst, src):
                sp.dma_start(dst, src).then_inc(S["ld_" + name], 16)

            sp.dma_start(x0[:, :, :], x_tiles[0]).then_inc(S["x_loaded"], 16)
            load("wqkv", wqkv[:, :], w["wqkv"])
            load("g", cols[:, 0:1], w["g"])
            load("b", cols[:, 1:2], w["b"])
            load("bq", cols[:, 2:3], w["bqkv"][0:D].rearrange("(p a) -> p a", a=1))
            load("bkv", bkv[:, :], w["bqkv"][D:3 * D].partition_broadcast(P))
            load("bout", bout[:, :], w["bout"].partition_broadcast(P))
            load("wout", wout[:, :], w["wout"])
            load("w1", mix[:, :, :], w["w1"].rearrange("p (e n) -> p e n", e=E))
            load("wr", lg[:, 0, :], w["wr"])
            load("br", br[:, :], w["br"].partition_broadcast(P))
            load("w2", work[:, 0:J * P], w["w2"])
            load("b1", b1[:, :], w["b1"])
            load("b2a", b2[0:E, :], w["b2"])
            load("b2b", b2[E:2 * E, :], w["b2"])
            load("wk", x2[:, 0, :], w["wk"])
            load("wq", x2[:, 1, :], w["wq"])
            load("wv", x2[:, 2, :], w["wv"])
            load("wo", wo[:, :], w["wo"])
            load("lnw", lnw[:, :], w["lnw"].partition_broadcast(P))
            sp.dma_start(lnb[:, :], w["lnb"].partition_broadcast(P)).then_inc(S["z_stored"], 16)

            def body(i, second, more):
                if more:
                    wait(sp, "x1_done", i, 1)
                    sp.dma_start(x0[:, :, :], x_tiles[i + 1]).then_inc(S["x_loaded"], 16)
                if second:
                    wait(sp, "z2_affine", i - 1, 2)
                    sp.dma_start(out_tiles[i - 1], z[:, :, :]).then_inc(S["z_stored"], 16)

            every_iteration(sp, body)
            wait(sp, "z_stored", B, 16)

        @block.gpsimd
        def _(gp):
            consts = [0]

            def const(ins):
                ins.then_inc(S["pool_const"], 1)
                consts[0] += 1
                gp.wait_ge(S["pool_const"], consts[0])

            def keep(ap, op, fill, base, pattern, mult):
                const(nc.gpsimd.affine_select(out=ap, in_=ap, compare_op=op, fill=fill, base=base,
                                              pattern=pattern, channel_multiplier=mult))

            const(nc.gpsimd.memset(ident[:, :], 0.0))
            keep(ident[:, :], ALU.not_equal, 1.0, 0, [[-1, P]], 1)
            const(nc.gpsimd.memset(head_mask[:, :], 0.0))
            hm = head_mask[:, :].rearrange("p (h e) -> p h e", e=HD)
            keep(hm, ALU.is_ge, NEG, 0, [[-HD, NH], [0, HD]], 1)
            keep(hm, ALU.is_ge, NEG, HD - 1, [[HD, NH], [0, HD]], -1)
            const(nc.gpsimd.memset(causal[:, :], 0.0))
            keep(causal[:, L - P:L], ALU.is_ge, NEG, 0, [[-1, P]], 1)
            const(nc.gpsimd.memset(ident_b[:, :], 0.0))
            keep(ident_b[:, :], ALU.not_equal, 1.0, 0, [[-1, P]], 1)
            const(nc.gpsimd.memset(later[:, :], 0.0))
            keep(later[:, :], ALU.is_ge, NEG, 0, [[1, P]], -1)
            const(nc.gpsimd.memset(minus_half[:, :], -0.5))
            const(nc.gpsimd.memset(base_e[:, :], 2.718281828459045))
            const(nc.gpsimd.iota(expert_id[:, :, :, :], [[0, T], [0, 2], [1, E]], base=0, channel_multiplier=0,
                                 allow_small_or_imprecise_dtypes=True))
            const(nc.gpsimd.memset(low_rows[:, :], 0.0))
            const(nc.gpsimd.memset(max_rows[:, :], 0.0))
            for j in range(4):
                for r in range(HD):
                    if r < 2:
                        keep(max_rows[:, 0:1], ALU.not_equal, 1.0, -(HS * j + 3 * HD + r), [[0, 1]], 1)
                    keep(low_rows[:, 0:1], ALU.not_equal, 1.0, -(HS * j + HD + r), [[0, 1]], 1)
                    keep(low_rows[:, 1:2], ALU.not_equal, 1.0, -(HS * j + 2 * HD + r), [[0, 1]], 1)
            for half in range(2):
                pk = (xnT, qT)[half]
                const(nc.gpsimd.memset(pk[0:2 * E, :], 0.0))
                pv = pk[0:2 * E, :].rearrange("p (e n) -> p e n", e=E // 2)
                for r in range(2):
                    keep(pv, ALU.not_equal, 1.0, -(half * E // 2 + r * E), [[-1, E // 2], [0, P]], 1)
            const(nc.gpsimd.memset(V[:, :, :, :], 0.0))
            const(nc.gpsimd.memset(V[:, :, :, HD:HD + 1], 1.0))
            const(nc.gpsimd.memset(spread[:, :, :], 0.0))

            def rstd(k, n, eps):
                st, mv, ve, rs = ln[k]
                wait(gp, k + "_moments", n, T)
                settle(gp)
                nc.gpsimd.tensor_scalar(ve[:, :], mv[:, :, 1], eps, None, ALU.add).then_inc(S[k + "_vareps"], 1)
                wait(gp, k + "_vareps", n, 1)
                nc.gpsimd.tensor_tensor(rs[:, :], ve[:, :], minus_half[:, :], ALU.pow).then_inc(S[k + "_rstd"], 1)

            def router(r, n):
                wait(gp, f"r{r}_pick", n, 10)
                nc.gpsimd.tensor_tensor(ratio[:, :], base_e[:, :], gap[:, :], ALU.pow).then_inc(S[f"r{r}_ratio"], 1)

            def moe_sum(n, e):
                wait(gp, "weighted_done", n, e + 1)
                if e > 1:
                    wait(gp, "summed", n, e - 1)
                nc.gpsimd.tensor_tensor(acc[:, :], acc[:, :], weighted[e % 2], ALU.add).then_inc(S["summed"], 1)

            def bias_x(s, xt, n):
                k = ("l1", "l3")[s]
                wait(gp, k + "_normed", n, T)
                nc.gpsimd.tensor_tensor(xt[:, :, :], xt[:, :, :], lnb[:, None, :].to_broadcast([P, T, D]),
                                        ALU.add).then_inc(S[f"x{2 * s + 1}_biased"], 1)

            def linear_1(n):
                rstd("la", n, 1e-5)
                wait(gp, "la_normed", n, T)
                nc.gpsimd.tensor_tensor(x0[:, :, :], x0[:, :, :], xa[:, :, :], ALU.add).then_inc(S["x0_sums"], 1)

            def linear_1b(n):
                rstd("lb", n, 1e-5)
                wait(gp, "x0_sums", n, 1)
                nc.gpsimd.tensor_tensor(x0[:, :, :], x0[:, :, :], bout[:, None, :].to_broadcast([P, T, D]),
                                        ALU.add).then_inc(S["x0_sums"], 1)

            def linear_2(n):
                rstd("l1", n, 1e-5)
                bias_x(0, x1, n)
                router(1, n)

            gp.wait_ge(S["ld_bout"], 16)
            wait(gp, "z_stored", 0, 16)
            linear_1(0)
            linear_1b(0)
            linear_2(0)

            def body(i, second, more):
                if not (isinstance(i, int) and i == B):
                    n1 = 2 * i - 1 if second else 0
                    for e in range(1, E):
                        if second and e == 1:
                            rstd("l3", i - 1, 1e-5)
                            bias_x(1, x3, i - 1)
                            router(2, i - 1)
                        moe_sum(n1, e)
                else:
                    rstd("l3", i - 1, 1e-5)
                    bias_x(1, x3, i - 1)
                    router(2, i - 1)
                if second:
                    n2 = 2 * i if not (isinstance(i, int) and i == B) else 2 * i - 1
                    last = isinstance(i, int) and i == B
                    for e in range(1, E):
                        if e == 1 and not last:
                            rstd("z1", i, 1e-12)
                            rstd("l2", i, 1e-5)
                        if e == 2 and more:
                            linear_1(i + 1)
                        if e == 3 and more:
                            linear_1b(i + 1)
                        moe_sum(n2, e)
                    if last:
                        rstd("z2", i - 1, 1e-12)
                        return
                else:
                    rstd("z1", i, 1e-12)
                    rstd("l2", i, 1e-5)
                    linear_1(i + 1)
                    linear_1b(i + 1)
                if second:
                    rstd("z2", i - 1, 1e-12)
                if more:
                    linear_2(i + 1)

            every_iteration(gp, body)

        @block.scalar
        def _(ac):
            def act(out_, in_, fn, name, **kw):
                return nc.scalar.activation(out_, in_, fn, **kw).then_inc(S[name], 1)

            def high_part(t, slot, n):
                wait(ac, f"t{t}_turned", n, 1)
                act(hh[slot][:, :], MISC[:, :], ACT.Copy, f"t{t}_high")

            def router(r, n):
                wait(ac, f"r{r}_turned", n, 1)
                act(cwT[r - 1][:, :], MISC[0:2 * E, :], ACT.Copy, f"r{r}_cwT")

            def mix_copy(r, n, e):
                wait(ac, f"r{r}_spread", n, e + 1)
                act(mix[:, e, :], MISC[:, :], ACT.Copy, f"r{r}_mix")

            def moe_gelu(n, j):
                wait(ac, "up_done", n, j + 1)
                wait(ac, "split_done", n, j - RG + 1)
                nc.scalar.activation(g32[j % RG], bank[j % 4][:, :], ACT.Gelu, bias=b1[:, j:j + 1])
                wait(ac, "down_done", n, j - RG + 1)
                act(gh[j % RG], bank[j % 4][:, :], ACT.Gelu, "gelu_done", bias=b1[:, j:j + 1])

            def moe(n, beside):
                for j in range(J):
                    moe_gelu(n, j)
                    beside(j)

            def linear_1(n):
                wait(ac, "xn_turned", n, 1)
                act(xnT[:, :], MISC[:, :], ACT.Identity, "xn_ready", scale=cols[:, 0:1], bias=cols[:, 1:2])
                wait(ac, "q_done", n, 1)
                act(qT[:, :], MISC[:, :], ACT.Identity, "q_biased", bias=cols[:, 2:3])

            def linear_2(n):
                wait(ac, "ktv_max", n, 2)
                act(sm[:, :], sm[:, :], ACT.Exp, "ktv_exp", bias=smx[:, 0:1], accum_out=smx[:, 1:2])
                wait(ac, "lin_mixed", n, 1)
                act(xnT[:, :], MISC[:, :], ACT.Copy, "lin_copied")

            for k in ("g", "b", "bq"):
                ac.wait_ge(S["ld_" + k], 16)
            ac.wait_ge(S["dve_const"], 2)
            linear_1(0)
            linear_2(0)
            high_part(1, 0, 0)
            router(1, 0)
            ac.wait_ge(S["w1_split"], 1)
            for e in range(E):
                mix_copy(1, 0, e)
            ac.wait_ge(S["ld_b1"], 16)
            ac.wait_ge(S["w2_split"], 1)

            def body(i, second, more):
                last = isinstance(i, int) and i == B

                def beside_1(j):
                    if not second:
                        return
                    if j == 5:
                        high_part(3, 1, i - 1)
                    if j == 9:
                        router(2, i - 1)
                    if j >= 12 and (j - 12) % 3 == 0 and (j - 12) // 3 < 6:
                        mix_copy(2, i - 1, (j - 12) // 3)

                def beside_2(j):
                    if j in (0, 1) and not last:
                        mix_copy(2, i - 1, 6 + j)
                    if j == 10 and not last:
                        high_part(2, 0, i)
                    if j == 20 and more:
                        linear_1(i + 1)

                if not last:
                    moe(2 * i - 1 if second else 0, beside_1)
                else:
                    high_part(3, 1, i - 1)
                    router(2, i - 1)
                    for e in range(E):
                        mix_copy(2, i - 1, e)
                if second:
                    moe(2 * i - 1 if last else 2 * i, beside_2)
                    if last:
                        return
                else:
                    high_part(2, 0, i)
                    linear_1(i + 1)
                for u in range(2 * NG):
                    g, s = u // 2, u % 2
                    wait(ac, "stack_mm", i, u + 1)
                    wait(ac, "stack_done", i, u - 1)
                    act(stack_low[u % 2], bank[u % 6][:, :], ACT.Copy, "stack_low", scale=low_rows[:, s:s + 1])
                wait(ac, "v_mm", i, 1)
                act(V[:, :, :, 0:HD], MISC[:, :].rearrange("p (t h d) -> p t h d", t=T, d=HD), ACT.Copy, "v_done")
                if more:
                    linear_2(i + 1)
                for s in range(NH + LAG):
                    if s >= LAG:
                        hd = s - LAG
                        if hd >= RP:
                            wait(ac, "pv_done", i, (hd - RP) // 4 + 1)
                        pr = work[:, (hd % RP) * PW:(hd % RP + 1) * PW]
                        for u, (lo, hi) in enumerate(((0, 512), (512, 1024), (1024, 1280))):
                            wait(ac, "pair_mm", i, 3 * hd + u + 1)
                            act(pr[:, lo:hi], bank[3 + u][:, 0:hi - lo], ACT.Exp, "exp_done", scale=SCALE)
                    if more:
                        if s == 4:
                            high_part(1, 0, i + 1)
                        if s == 7:
                            router(1, i + 1)
                        if s >= 8 and s < 16:
                            mix_copy(1, i + 1, s - 8)
                    if s >= LAG + 5 and (s - LAG - 5) % 4 == 0:
                        g = (s - LAG - 5) // 4
                        wait(ac, "pv_done", i, g + 1)
                        wait(ac, "pv_turned", i, g)
                        act(oT[:, :], PV[:, :], ACT.Copy, "pv_copied")
                wait(ac, "pv_done", i, NG)
                wait(ac, "pv_turned", i, NG - 1)
                act(oT[:, :], PV[:, :], ACT.Copy, "pv_copied")
                wait(ac, "o_turned", i, 1)
                act(oT[:, :], MISC[:, :], ACT.Copy, "o_copied")

            every_iteration(ac, body)

        @block.vector
        def _(ve):
            def stats(k, src, n, ready=None):
                st, mv, _, _ = ln[k]
                for t in range(T):
                    if ready is not None:
                        ready(t)
                    nc.vector.bn_stats(st[:, t, :], src[:, t, :]).then_inc(S[k + "_stats"], 1)
                wait(ve, k + "_stats", n, T)
                settle(ve)
                for t in range(T):
                    nc.vector.bn_aggr(mv[:, t, :], st[:, t, :]).then_inc(S[k + "_moments"], 1)

            def norm(k, dst, src, n):
                st, mv, _, rs = ln[k]
                wait(ve, k + "_rstd", n, 1)
                for t in range(T):
                    nc.vector.tensor_scalar(dst[:, t, :], src[:, t, :], mv[:, t, 0:1], rs[:, t:t + 1],
                                            ALU.subtract, ALU.mult).then_inc(S[k + "_normed"], 1)

            def split(hi, lo, src, ready):
                nc.vector.tensor_copy(hi, src).then_inc(S["dve_const"], 1)
                split.n += 1
                ve.wait_ge(S["dve_const"], split.n)
                nc.vector.tensor_tensor(lo, src, hi.bitcast(F32), ALU.subtract).then_inc(S["dve_const"], 1)
                split.n += 1

            def low_part(t, slot, n):
                wait(ve, f"t{t}_high", n, 1)
                nc.vector.tensor_tensor(hl[slot][:, :], MISC[:, :], hh[slot][:, :].bitcast(F32),
                                        ALU.subtract).then_inc(S[f"t{t}_low"], 1)

            def router_1(r, n):
                k = f"r{r}_pick"
                wait(ve, f"r{r}_logits", n, 1)
                nc.vector.tensor_tensor(lg[:, :, :], MISC[:, 0:T * E].rearrange("p (t e) -> p t e", e=E),
                                        br[:, None, :].to_broadcast([P, T, E]), ALU.add).then_inc(S[k], 1)
                wait(ve, k, n, 1)
                settle(ve)
                for t in range(T):
                    nc.vector.max(top[:, t, :], lg[:, t, :]).then_inc(S[k], 1)
                wait(ve, k, n, 5)
                nc.vector.tensor_tensor(gap[:, :], top[:, :, 1], top[:, :, 0], ALU.subtract).then_inc(S[k], 1)
                for t in range(T):
                    nc.vector.max_index(topi[:, t, :], top[:, t, :], lg[:, t, :]).then_inc(S[k], 1)

            def router_2(r, n):
                k = f"r{r}_share"
                wait(ve, f"r{r}_pick", n, 10)
                nc.vector.tensor_copy(topf[:, :, :], topi[:, :, 0:2]).then_inc(S[k], 1)
                wait(ve, f"r{r}_ratio", n, 1)
                nc.vector.tensor_scalar(one_more[:, :], ratio[:, :], 1.0, None, ALU.add).then_inc(S[k], 1)
                wait(ve, k, n, 2)
                nc.vector.reciprocal(share[:, :, 0], one_more[:, :]).then_inc(S[k], 1)
                nc.vector.tensor_tensor(chosen[:, :, :, :], expert_id[:, :, :, :],
                                        topf[:, :, :, None].to_broadcast([P, T, 2, E]),
                                        ALU.is_equal).then_inc(S[k], 1)
                wait(ve, k, n, 4)
                nc.vector.tensor_tensor(share[:, :, 1], share[:, :, 0], ratio[:, :], ALU.mult).then_inc(S[k], 1)
                wait(ve, k, n, 5)
                nc.vector.tensor_tensor(chosen[:, :, :, :], chosen[:, :, :, :],
                                        share[:, :, :, None].to_broadcast([P, T, 2, E]),
                                        ALU.mult).then_inc(S[k], 1)
                wait(ve, k, n, 6)
                nc.vector.tensor_tensor(cw[:, :, :], chosen[:, :, 0, :], chosen[:, :, 1, :], ALU.add).then_inc(S[k], 1)
                wait(ve, k, n, 7)
                nc.vector.tensor_copy(cwp[:, :, 0:E].bitcast(F32R), cw[:, :, :]).then_inc(S[k], 1)
                wait(ve, k, n, 8)
                nc.vector.tensor_tensor(cwp[:, :, E:2 * E], cw[:, :, :], cwp[:, :, 0:E], ALU.subtract).then_inc(S[k], 1)

            def moe_split(n, j):
                wait(ve, "gelu_done", n, j + 1)
                wait(ve, "down_done", n, j - RG + 1)
                nc.vector.tensor_tensor(gl[j % RG], g32[j % RG], gh[j % RG].bitcast(F32),
                                        ALU.subtract).then_inc(S["split_done"], 1)

            def moe_weigh(n, e):
                wait(ve, "down_done", n, FT * e + FT)
                if e >= 2:
                    wait(ve, "summed", n, e - 2)
                nc.vector.tensor_tensor(acc[:, :] if e == 0 else weighted[e % 2], bank[4 + e % 2][:, :],
                                        mix[:, e, :], ALU.mult).then_inc(S["weighted_done"], 1)

            def moe(n, first_e, beside):
                for j in range(J):
                    moe_split(n, j)
                    if j >= 5 and (j - 5) % FT == 0:
                        if j == 5:
                            first_e()
                        moe_weigh(n, (j - 5) // FT)
                    beside(j)
                moe_weigh(n, E - 1)

            def end_moe_1(s, n, z_free):
                wait(ve, f"z{s}_back", n, 1)
                wait(ve, *z_free)
                nc.vector.tensor_tensor(z[:, :, :], MISC[:, :].rearrange("p (t d) -> p t d", t=T), h[s - 1][:, :, :],
                                        ALU.add).then_inc(S[f"z{s}_resid"], 1)
                wait(ve, f"z{s}_resid", n, 1)
                stats(f"z{s}", z, n)

            def end_moe_2(s, n, xin, dst):
                norm(f"z{s}", z, z, n)
                wait(ve, f"z{s}_normed", n, T)
                nc.vector.tensor_tensor(z[:, :, :], z[:, :, :], lnw[:, None, :].to_broadcast([P, T, D]),
                                        ALU.mult).then_inc(S[f"z{s}_affine"], 1)
                wait(ve, f"z{s}_affine", n, 1)
                wait(ve, f"x{2 * s - 1}_biased", n, 1)
                nc.vector.tensor_tensor(dst[:, :, :], z[:, :, :], xin[:, :, :], ALU.add).then_inc(S[f"z{s}_affine"], 1)

            def linear_1a(n):
                wait(ve, "x_loaded", n, 16)
                stats("la", x0, n)
                norm("la", xa, x0, n)

            def linear_1b(n):
                stats("lb", xa, n, lambda t: wait(ve, "la_normed", n, t + 1))
                norm("lb", nrm, xa, n)

            def linear_1c(n):
                for c in range(2):
                    wait(ve, "kv_done", n, c + 1)
                    nc.vector.tensor_tensor(kv[:, 2 * c:2 * c + 2, :], MISC[:, :].rearrange("p (t d) -> p t d", t=2),
                                            bkv[:, None, :].to_broadcast([P, 2, 2 * D]),
                                            ALU.add).then_inc(S["kv_biased"], 1)
                wait(ve, "ktv_done", n, 1)
                nc.vector.tensor_tensor(sm[:, :], MISC[:, 0:P], head_mask[:, :], ALU.add).then_inc(S["ktv_max"], 1)
                wait(ve, "ktv_max", n, 1)
                nc.vector.tensor_reduce(smx[:, 0:1], sm[:, :], AX.X, ALU.max, negate=True).then_inc(S["ktv_max"], 1)

            def linear_2a(n):
                wait(ve, "ktv_exp", n, 1)
                nc.vector.reciprocal(smx[:, 2:3], smx[:, 1:2]).then_inc(S["ktv_soft"], 1)
                wait(ve, "ktv_soft", n, 1)
                nc.vector.tensor_scalar(sm[:, :], sm[:, :], smx[:, 2:3], None, ALU.mult).then_inc(S["ktv_soft"], 1)

            def linear_2b(n):
                wait(ve, "lin_out", n, 1)
                wait(ve, "x0_sums", n, 2)
                nc.vector.tensor_tensor(x1[:, :, :], MISC[:, :].rearrange("p (t d) -> p t d", t=T), x0[:, :, :],
                                        ALU.add).then_inc(S["x1_done"], 1)
                wait(ve, "x1_done", n, 1)
                stats("l1", x1, n)

            split.n = 0
            ve.wait_ge(S["pool_const"], POOL_CONSTS)
            nc.vector.tensor_copy(pick[:, 0:E // 2, :], xnT[0:2 * E, :].rearrange("p (e n) -> p e n", n=P)).then_inc(S["dve_const"], 1)
            nc.vector.tensor_copy(pick[:, E // 2:E, :], qT[0:2 * E, :].rearrange("p (e n) -> p e n", n=P)).then_inc(S["dve_const"], 1)
            split.n = 2
            for k in ("bkv", "wr", "br"):
                ve.wait_ge(S["ld_" + k], 16)
            split(wrh[:, :], wrl[:, :], lg[:, 0, :], None)
            ve.wait_ge(S["dve_const"], split.n)
            linear_1a(0)
            linear_1b(0)
            linear_1c(0)
            linear_2a(0)
            linear_2b(0)
            norm("l1", h[0], x1, 0)
            low_part(1, 0, 0)
            router_1(1, 0)
            router_2(1, 0)
            ve.wait_ge(S["ld_w1"], 16)
            split(w1h[:, :], w1l[:, :], mix[:, :, :].rearrange("p e n -> p (e n)"), None)
            ve.wait_ge(S["dve_const"], split.n)
            nc.vector.memset(smx[:, 3:4], 0.0).then_inc(S["w1_split"], 1)
            ve.wait_ge(S["ld_w2"], 16)
            split(w2h[:, :], w2l[:, :], work[:, 0:J * P], None)
            ve.wait_ge(S["dve_const"], split.n)
            ve.wait_ge(S["w1_split"], 1)
            nc.vector.memset(smx[:, 3:4], 0.0).then_inc(S["w2_split"], 1)
            for k in ("wk", "wq", "wv", "lnw"):
                ve.wait_ge(S["ld_" + k], 16)
            for s in range(2):
                dst = x3[:, :, :].rearrange("p t (g r) -> p (t g) r", r=HS)
                src = x2[:, s, :].rearrange("p (h d) -> p h d", d=HD)
                nc.vector.memset(x3[:, :, :], 0.0).then_inc(S["dve_const"], 1)
                split.n += 1
                ve.wait_ge(S["dve_const"], split.n)
                for r in range(3):
                    nc.vector.tensor_copy(dst[:, :, r * HD:(r + 1) * HD], src).then_inc(S["dve_const"], 1)
                    split.n += 1
                ve.wait_ge(S["dve_const"], split.n)
                split(wsh[:, s, :], wsl[:, s, :], x3[:, :, :].rearrange("p t n -> p (t n)"), None)
                ve.wait_ge(S["dve_const"], split.n)
            split(wvh[:, :], wvl[:, :], x2[:, 2, :], None)
            ve.wait_ge(S["dve_const"], split.n)
            assert split.n == DVE_CONSTS

            def body(i, second, more):
                last = isinstance(i, int) and i == B

                def beside_1(j):
                    if not second:
                        return
                    if j == 0:
                        stats("l3", x3, i - 1)
                    if j == 2:
                        norm("l3", h[1], x3, i - 1)
                    if j == 5:
                        low_part(3, 1, i - 1)
                    if j == 6:
                        router_1(2, i - 1)
                    if j == 8:
                        router_2(2, i - 1)

                def beside_2(j):
                    if last:
                        return
                    if j == 1:
                        end_moe_1(1, i, ("z_stored", i, 0))
                    if j == 3:
                        end_moe_2(1, i, x1, x2)
                        wait(ve, "z1_affine", i, 2)
                        stats("l2", x2, i)
                    if j == 6:
                        wait(ve, "xn_turned", i, 1)
                        norm("l2", nrm, x2, i)
                    if j == 10:
                        low_part(2, 0, i)
                    if more:
                        if j == 12:
                            linear_1a(i + 1)
                        if j == 14:
                            stats("lb", xa, i + 1, lambda t: wait(ve, "la_normed", i + 1, t + 1))
                        if j == 16:
                            wait(ve, "t2_turned", i, 1)
                            norm("lb", nrm, xa, i + 1)
                        if j == 20:
                            linear_1c(i + 1)

                if not last:
                    if second:
                        wait(ve, "x3_done", i - 1, 1)
                    moe(2 * i - 1 if second else 0, lambda: wait(ve, "z2_back", i - 2, 1) if False else None, beside_1)
                else:
                    wait(ve, "x3_done", i - 1, 1)
                    stats("l3", x3, i - 1)
                    norm("l3", h[1], x3, i - 1)
                    low_part(3, 1, i - 1)
                    router_1(2, i - 1)
                    router_2(2, i - 1)
                if second:
                    moe(2 * i - 1 if last else 2 * i,
                        (lambda: None) if last else (lambda: wait(ve, "z1_back", i, 1)), beside_2)
                else:
                    end_moe_1(1, i, ("z_stored", i, 0))
                    end_moe_2(1, i, x1, x2)
                    wait(ve, "z1_affine", i, 2)
                    stats("l2", x2, i)
                    norm("l2", nrm, x2, i)
                    low_part(2, 0, i)
                    linear_1a(i + 1)
                    stats("lb", xa, i + 1, lambda t: wait(ve, "la_normed", i + 1, t + 1))
                    wait(ve, "t2_turned", i, 1)
                    norm("lb", nrm, xa, i + 1)
                    linear_1c(i + 1)
                if last:
                    end_moe_1(2, i - 1, ("z_stored", i - 1, 16))
                    end_moe_2(2, i - 1, x3, z)
                    return
                for u in range(2 * NG):
                    g, s = u // 2, u % 2
                    wait(ve, "stack_low", i, u + 1)
                    nc.vector.scalar_tensor_tensor(
                        out=stack[g][s], in0=bank[u % 6][:, :], scalar=max_rows[:, s:s + 1],
                        in1=stack_low[u % 2].bitcast(F32), op0=ALU.add, op1=ALU.subtract,
                    ).then_inc(S["stack_done"], 1)
                if second:
                    end_moe_1(2, i - 1, ("z1_affine", i, 2))
                if more:
                    linear_2a(i + 1)
                for s in range(NH + LAG):
                    if s < NH:
                        g, j = s // 4, s % 4
                        for k, qt in enumerate((3, 2, 0, 1)):
                            b_, c = Q_BANK[qt]
                            n_ = (qt + 1) * P
                            wait(ve, "logit_mm", i, 3 * s + b_ + 1)
                            wait(ve, "max_done", i, 4 * s + k - 1)
                            settle(ve)
                            nc.vector.tensor_tensor_reduce(
                                junk[:, k % 2, 0:n_], bank[b_][:, c:c + n_], causal[:, L - n_:L], 1.0, NEG,
                                ALU.add, ALU.max, hmax[:, g, j, qt:qt + 1]).then_inc(S["max_done"], 1)
                        if j == 3:
                            src = hmax[:, g, :, :].rearrange("p j t -> p t j")
                            dst = spread[:, :, :].rearrange("p t (j r) -> p t j r", r=HS)
                            wait(ve, "max_done", i, 4 * s + 4)
                            wait(ve, "max_turned", i, g)
                            nc.vector.tensor_copy(dst[:, :, :, 3 * HD].bitcast(F32R), src).then_inc(S["max_spread"], 1)
                            wait(ve, "max_spread", i, 2 * g + 1)
                            nc.vector.tensor_tensor(dst[:, :, :, 3 * HD + 1], src, dst[:, :, :, 3 * HD],
                                                    ALU.subtract).then_inc(S["max_spread"], 1)
                    if s >= 5 and (s - 5) % 4 == 0 and (s - 5) // 4 < NG:
                        g = (s - 5) // 4
                        wait(ve, "max_turned", i, g + 1)
                        nc.vector.tensor_tensor(stack[g][1], stack[g][1].bitcast(F32), MISC[:, :],
                                                ALU.subtract).then_inc(S["max_in_q"], 1)
                    if second:
                        if s == 2:
                            end_moe_2(2, i - 1, x3, z)
                    if more:
                        if s == 2:
                            linear_2b(i + 1)
                        if s == 3:
                            norm("l1", h[0], x1, i + 1)
                        if s == 4:
                            low_part(1, 0, i + 1)
                        if s == 5:
                            router_1(1, i + 1)
                        if s == 6:
                            router_2(1, i + 1)
                    if s >= LAG + 6 and (s - LAG - 6) % 4 == 0:
                        normalize(i, (s - LAG - 6) // 4)
                normalize(i, NG - 1)
                wait(ve, "wo_done", i, 1)
                nc.vector.tensor_tensor(x3[:, :, :], MISC[:, :].rearrange("p (t d) -> p t d", t=T), x2[:, :, :],
                                        ALU.add).then_inc(S["x3_done"], 1)

            def normalize(i, g):
                wait(ve, "pv_turned", i, g + 1)
                if g > 0:
                    wait(ve, "o_normed", i, g)
                elif True:
                    wait(ve, "o_normed", i, 0)
                src = MISC[:, :].rearrange("p (t j r) -> p t j r", t=T, r=HS)
                nc.vector.reciprocal(inv[:, :, :], src[:, :, :, HD]).then_inc(S["inv_done"], 1)
                wait(ve, "inv_done", i, g + 1)
                nc.vector.tensor_tensor(
                    o[:, :, :].rearrange("p t (g j d) -> p t g j d", g=NG, d=HD)[:, :, g], src[:, :, :, 0:HD],
                    inv[:, :, :, None].to_broadcast([P, T, 4, HD]), ALU.mult).then_inc(S["o_normed"], 1)

            every_iteration(ve, body)

        @block.tensor
        def _(pe):
            read_by = [None]

            def misc_free(reader):
                if read_by[0] is not None:
                    wait(pe, *read_by[0])
                read_by[0] = reader

            def turn(src, ready, name, n, reader):
                misc_free(reader)
                for t in range(T):
                    ready(t)
                    ins = nc.tensor.transpose(MISC[:, t * P:(t + 1) * P], src[:, t, :], ident[:, :])
                ins.then_inc(S[name], 1)

            def three(dst, ah, al, bh, bl, start=True, stop=True):
                nc.tensor.matmul(dst, ah, bh, start=start, stop=False)
                nc.tensor.matmul(dst, al, bh, start=False, stop=False)
                return nc.tensor.matmul(dst, ah, bl, start=False, stop=stop)

            def moe_up(n, j, slot):
                c = slice(j * P, (j + 1) * P)
                wait(pe, "gelu_done", n, j - 3)
                three(bank[j % 4][:, :], w1h[:, c], w1l[:, c], hh[slot][:, :], hl[slot][:, :]).then_inc(S["up_done"], 1)

            def moe_down(n, j):
                e, f = j // FT, j % FT
                c = slice(j * P, (j + 1) * P)
                wait(pe, "split_done", n, j + 1)
                if f == 0:
                    wait(pe, "weighted_done", n, e - 1)
                three(bank[4 + e % 2][:, :], w2h[:, c], w2l[:, c], gh[j % RG], gl[j % RG],
                      start=f == 0, stop=f == FT - 1).then_inc(S["down_done"], 1)

            def moe(n, slot, beside):
                for j in range(3):
                    moe_up(n, j, slot)
                for j in range(J):
                    moe_down(n, j)
                    if j + 3 < J:
                        moe_up(n, j + 3, slot)
                    beside(j)

            def moe_back(s, n, nmoe):
                misc_free((f"z{s}_resid", n, 1))
                wait(pe, "summed", nmoe, E - 1)
                for t in range(T):
                    c = slice(t * P, (t + 1) * P)
                    nc.tensor.matmul(MISC[:, c], acc[:, c], ident[:, :], start=True, stop=False)
                    ins = nc.tensor.matmul(MISC[:, c], cwT[s - 1][:, c].bitcast(F32), b2[:, :], start=False, stop=True)
                ins.then_inc(S[f"z{s}_back"], 1)

            def router_1(r, slot, t_, n):
                misc_free((f"r{r}_pick", n, 1))
                for t in range(T):
                    c = slice(t * P, (t + 1) * P)
                    ins = three(MISC[:, t * E:(t + 1) * E], hh[slot][:, c], hl[slot][:, c], wrh[:, :], wrl[:, :])
                ins.then_inc(S[f"r{r}_logits"], 1)

            def router_2(r, n):
                misc_free((f"r{r}_cwT", n, 1))
                wait(pe, f"r{r}_share", n, 9)
                for t in range(T):
                    ins = nc.tensor.transpose(MISC[0:2 * E, t * P:(t + 1) * P], cwp[:, t, :], ident[:, :])
                ins.then_inc(S[f"r{r}_turned"], 1)

            def spread_mix(r, n, e):
                misc_free((f"r{r}_mix", n, e + 1))
                wait(pe, f"r{r}_cwT", n, 1)
                nc.tensor.matmul(MISC[:, :], pick[:, e, :], cwT[r - 1][:, :], start=True, stop=True
                                 ).then_inc(S[f"r{r}_spread"], 1)

            def linear_1a(n):
                turn(nrm, lambda t: wait(pe, "lb_normed", n, t + 1), "xn_turned", n, ("xn_ready", n, 1))

            def linear_1b(n):
                for c in range(2):
                    misc_free(("kv_biased", n, c + 1))
                    if c == 0:
                        wait(pe, "xn_ready", n, 1)
                    for t in range(2 * c, 2 * c + 2):
                        ins = nc.tensor.matmul(MISC[:, (t % 2) * 2 * D:(t % 2 + 1) * 2 * D], xnT[:, t * P:(t + 1) * P],
                                               wqkv[:, D:3 * D], start=True, stop=True)
                    ins.then_inc(S["kv_done"], 1)
                misc_free(("q_biased", n, 1))
                nc.tensor.matmul(MISC[:, :], wqkv[:, 0:D], xnT[:, :], start=True, stop=True).then_inc(S["q_done"], 1)
                misc_free(("ktv_max", n, 1))
                wait(pe, "kv_biased", n, 2)
                for t in range(T):
                    ins = nc.tensor.matmul(MISC[:, 0:P], kv[:, t, 0:D], kv[:, t, D:2 * D], start=t == 0, stop=t == T - 1)
                ins.then_inc(S["ktv_done"], 1)

            def linear_2a(n):
                misc_free(("lin_copied", n, 1))
                wait(pe, "ktv_soft", n, 2)
                nc.tensor.matmul(MISC[:, :], sm[:, :], qT[:, :], start=True, stop=True).then_inc(S["lin_mixed"], 1)

            def linear_2b(n):
                misc_free(("x1_done", n, 1))
                for t in range(T):
                    c = slice(t * P, (t + 1) * P)
                    ins = nc.tensor.matmul(MISC[:, c], xnT[:, c], wout[:, :], start=True, stop=True)
                ins.then_inc(S["lin_out"], 1)

            pe.wait_ge(S["pool_const"], POOL_CONSTS)
            pe.wait_ge(S["ld_wqkv"], 16)
            pe.wait_ge(S["ld_wout"], 16)
            linear_1a(0)
            linear_1b(0)
            linear_2a(0)
            linear_2b(0)
            turn(h[0], lambda t: wait(pe, "l1_normed", 0, t + 1), "t1_turned", 0, ("t1_low", 0, 1))
            pe.wait_ge(S["dve_const"], 4)
            router_1(1, 0, 1, 0)
            router_2(1, 0)
            for e in range(E):
                spread_mix(1, 0, e)
            for k in ("b2a", "b2b", "wo"):
                pe.wait_ge(S["ld_" + k], 16)
            pe.wait_ge(S["dve_const"], DVE_CONSTS)

            def body(i, second, more):
                last = isinstance(i, int) and i == B
                if second:
                    read_by[0] = ("x3_done", i - 1, 1)

                def beside_1(j):
                    if not second:
                        return
                    n = i - 1
                    if j == 4:
                        turn(h[1], lambda t: wait(pe, "l3_normed", n, t + 1), "t3_turned", n, ("t3_low", n, 1))
                    if j == 6:
                        router_1(2, 1, 3, n)
                    if j == 9:
                        router_2(2, n)
                    if j >= 12 and (j - 12) % 3 == 0 and (j - 12) // 3 < 6:
                        e = (j - 12) // 3
                        wait(pe, "weighted_done", 2 * i - 1, e + 1)
                        spread_mix(2, n, e)

                def beside_2(j):
                    if last:
                        return
                    if j in (0, 1):
                        spread_mix(2, i - 1, 6 + j)
                    if j == 1:
                        moe_back(1, i, 2 * i - 1)
                    if j == 9:
                        turn(nrm, lambda t: wait(pe, "l2_normed", i, t + 1), "t2_turned", i, ("t2_low", i, 1))
                    if more:
                        if j == 19:
                            linear_1a(i + 1)
                        if j == 20:
                            linear_1b(i + 1)

                if not last:
                    if second:
                        wait(pe, "max_done", i - 1, 4 * NH)
                        wait(pe, "exp_done", i - 1, 3 * NH)
                    moe(2 * i - 1 if second else 0, 0, beside_1)
                else:
                    n = i - 1
                    turn(h[1], lambda t: wait(pe, "l3_normed", n, t + 1), "t3_turned", n, ("t3_low", n, 1))
                    router_1(2, 1, 3, n)
                    router_2(2, n)
                    for e in range(E):
                        spread_mix(2, n, e)
                if second:
                    if last:
                        wait(pe, "max_done", i - 1, 4 * NH)
                        wait(pe, "exp_done", i - 1, 3 * NH)
                    moe(2 * i - 1 if last else 2 * i, 1, beside_2)
                else:
                    moe_back(1, i, 0)
                    turn(nrm, lambda t: wait(pe, "l2_normed", i, t + 1), "t2_turned", i, ("t2_low", i, 1))
                    linear_1a(i + 1)
                    linear_1b(i + 1)
                if last:
                    moe_back(2, i - 1, 2 * i - 1)
                    return
                nmoe = 2 * i if second else 0
                wait(pe, "gelu_done", nmoe, J)
                wait(pe, "weighted_done", nmoe, E)
                for u in range(2 * NG):
                    g, s = u // 2, u % 2
                    c = slice(g * P, (g + 1) * P)
                    wait(pe, "stack_done", i, u - 5)
                    if u == 0:
                        wait(pe, "t2_low", i, 1)
                    three(bank[u % 6][:, :], wsh[:, s, c], wsl[:, s, c], hh[0][:, :], hl[0][:, :]
                          ).then_inc(S["stack_mm"], 1)
                misc_free(("v_done", i, 1))
                for t in range(T):
                    c = slice(t * P, (t + 1) * P)
                    ins = three(MISC[:, c], hh[0][:, c], hl[0][:, c], wvh[:, :], wvl[:, :])
                ins.then_inc(S["v_mm"], 1)
                if second:
                    moe_back(2, i - 1, 2 * i)
                if more:
                    linear_2a(i + 1)
                for s in range(NH + LAG):
                    if s < NH:
                        g, rows = s // 4, slice((s % 4) * HS, (s % 4 + 1) * HS)
                        if s == 0:
                            wait(pe, "stack_done", i, 2 * NG)
                        for b_, tiles in enumerate(((3,), (2, 0), (1,))):
                            wait(pe, "max_done", i, 4 * (s - 1) + (1, 3, 4)[b_])
                            for qt in tiles:
                                c0 = Q_BANK[qt][1]
                                ins = nc.tensor.matmul(
                                    bank[b_][:, c0:c0 + (qt + 1) * P], stack[g][1][rows, qt * P:(qt + 1) * P],
                                    stack[g][0][rows, 0:(qt + 1) * P], start=True, stop=True)
                            ins.then_inc(S["logit_mm"], 1)
                    if s >= 5 and (s - 5) % 4 == 0 and (s - 5) // 4 < NG:
                        g = (s - 5) // 4
                        turn(spread, lambda t: wait(pe, "max_spread", i, 2 * g + 2) if t == 0 else None,
                             "max_turned", i, ("max_in_q", i, g + 1))
                    if s >= LAG:
                        hd = s - LAG
                        g, rows = hd // 4, slice((hd % 4) * HS, (hd % 4 + 1) * HS)
                        wait(pe, "max_in_q", i, g + 1)
                        for u, tiles in enumerate(((0,), (1, 3), (2,))):
                            wait(pe, "exp_done", i, 3 * (hd - 1) + u + 1)
                            for kt in tiles:
                                b_, c0 = K_BANK[kt]
                                nc.tensor.matmul(
                                    bank[b_][:, c0:c0 + L - kt * P], stack[g][0][rows, kt * P:(kt + 1) * P],
                                    stack[g][1][rows, kt * P:L], start=True, stop=False)
                                ins = nc.tensor.matmul(bank[b_][:, c0:c0 + P], ident_b[:, :], later[:, :],
                                                       start=False, stop=True)
                            ins.then_inc(S["pair_mm"], 1)
                    if more:
                        n = i + 1
                        if s == 1:
                            linear_2b(n)
                        if s == 4:
                            turn(h[0], lambda t: wait(pe, "l1_normed", n, t + 1), "t1_turned", n, ("t1_low", n, 1))
                        if s == 5:
                            router_1(1, 0, 1, n)
                        if s == 7:
                            router_2(1, n)
                        if 8 <= s < 16:
                            spread_mix(1, n, s - 8)
                    if s >= LAG + 4 and (s - LAG - 4) % 4 == 0:
                        values(i, (s - LAG - 4) // 4)
                    if s >= LAG + 6 and (s - LAG - 6) % 4 == 0:
                        values_back(i, (s - LAG - 6) // 4)
                values(i, NG - 1)
                values_back(i, NG - 1)
                turn(o, lambda t: wait(pe, "o_normed", i, NG) if t == 0 else None, "o_turned", i, ("o_copied", i, 1))
                misc_free(("x3_done", i, 1))
                for t in range(T):
                    c = slice(t * P, (t + 1) * P)
                    ins = nc.tensor.matmul(MISC[:, c], oT[:, c], wo[:, :], start=True, stop=True)
                ins.then_inc(S["wo_done"], 1)

            def values(i, g):
                wait(pe, "v_done", i, 1)
                wait(pe, "pv_copied", i, g)
                wait(pe, "exp_done", i, 3 * (4 * g + 4))
                for kt in range(T):
                    for j in range(4):
                        hd = 4 * g + j
                        a = (hd % RP) * PW + K_OFF[kt]
                        ins = nc.tensor.matmul(PV[j * HS:(j + 1) * HS, kt * P:L], V[:, kt, hd, :],
                                               work[:, a:a + L - kt * P], start=kt == 0, stop=kt == T - 1,
                                               skip_group_check=True)
                ins.then_inc(S["pv_done"], 1)

            def values_back(i, g):
                misc_free(("o_normed", i, g + 1))
                wait(pe, "pv_copied", i, g + 1)
                for t in range(T):
                    ins = nc.tensor.transpose(MISC[:, t * P:(t + 1) * P], oT[:, t * P:(t + 1) * P], ident[:, :])
                ins.then_inc(S["pv_turned"], 1)

            every_iteration(pe, body)


POOL_CONSTS = 9 + 2 + 3 + 2 + 4 * (2 + 8 + 8) + 6 + 3
DVE_CONSTS = 2 + 2 + 4 + 2 * (4 + 2) + 2


def kernel(**a):
    import numpy as np
    import concourse.bacc as bacc
    from concourse.bass_utils import run_bass_kernel_spmd

    def f(name):
        return np.asarray(a[name])

    def c(v):
        return np.ascontiguousarray(v)

    w1, w2 = f("L0_ffn_W1"), f("L0_ffn_W2")
    laid = {
        "x": c(f("L0_attn_a_x")),
        "wqkv": c(f("L0_attn_a_w_qkv")),
        "bqkv": c(f("L0_attn_a_b_qkv")),
        "wout": c(f("L0_attn_a_w_out")),
        "bout": c(f("L0_attn_a_b_out")),
        "g": c(f("L0_attn_a_ln_g").reshape(P, 1)),
        "b": c(f("L0_attn_a_ln_b").reshape(P, 1)),
        "wq": c(f("L0_attn_b_Wq").T),
        "wk": c(f("L0_attn_b_Wk").T),
        "wv": c(f("L0_attn_b_Wv").T),
        "wo": c(f("L0_attn_b_Wo").T),
        "wr": c(f("L0_ffn_Wr").T),
        "br": c(f("L0_ffn_br")),
        "w1": c(w1.reshape(E * F, D).T),
        "b1": c(f("L0_ffn_b1").reshape(J, P).T),
        "w2": c(w2.reshape(E, D, FT, P).transpose(3, 0, 2, 1).reshape(P, J * D)),
        "b2": c(f("L0_ffn_b2")),
        "lnw": c(f("L0_ffn_ln_w")),
        "lnb": c(f("L0_ffn_ln_b")),
    }
    nc = bacc.Bacc("TRN2", target_bir_lowering=False, num_devices=1)
    w = {k: nc.dram_tensor(f"in_{k}", v.shape, mybir.dt.from_np(v.dtype), kind="ExternalInput").ap()
         for k, v in laid.items()}
    out = nc.dram_tensor("out", (B, L, D), F32, kind="ExternalOutput").ap()
    build(nc, w["x"], out, w)
    r = run_bass_kernel_spmd(nc, [{f"in_{k}": v for k, v in laid.items()}], core_ids=[0])
    return r.results[0]["out"]
```

```python
from contextlib import ExitStack

import concourse.bass as bass
import concourse.mybir as mybir
from concourse.alu_op_type import AluOpType as ALU

F32 = mybir.dt.float32
F32R = mybir.dt.float32r
BF16 = mybir.dt.bfloat16
U32 = mybir.dt.uint32
ACT = mybir.ActivationFunctionType
AX = mybir.AxisListType

P = 128
B, L, D = 8, 512, 128
T = L // P
NH, HD = 16, 8
HS = 32
NG = NH // 4
E, F = 8, 512
FT = F // P
J = E * FT
RG = 3
RP = 5
PW = 1280
LAG = 6
NEG = -3.0e38
SCALE = float(HD) ** -0.5
K_OFF = [0, 512, 1024, 896]
K_BANK = [(3, 0), (4, 0), (5, 0), (4, 384)]
Q_BANK = [(1, 384), (2, 0), (1, 0), (0, 0)]

BY_ACT = {1: [0], 2: [0, 2, 5, 6]}
BY_DVE = {1: [1, 2, 3, 4, 5, 6, 7], 2: [1, 3, 4, 7]}

PER = {}


def at(name, n, k):
    return PER[name] * n + k


def mix_done(r, e):
    for name, experts in (("act", BY_ACT[r]), ("dve", BY_DVE[r])):
        if e in experts:
            return f"r{r}_mix_{name}", experts.index(e) + 1


def build(nc, x, out, w):
    ctx = ExitStack()
    with ctx:
        def sb(name, shape, dt=F32):
            return ctx.enter_context(nc.sbuf_tensor(name, shape, dt))

        S = {}

        def sem(name, per):
            S[name] = ctx.enter_context(nc.semaphore(name))
            PER[name] = per

        def wait(eng, name, n, k):
            v = at(name, n, k)
            if not isinstance(v, int) or v > 0:
                eng.wait_ge(S[name], v)

        def settle(eng):
            eng.nop(nofuse=True)

        ident = sb("ident", [P, P])
        head_mask = sb("head_mask", [P, P])
        causal = sb("causal", [P, L])
        ident_b = sb("ident_b", [P, P], BF16)
        later = sb("later", [P, P], BF16)
        expert_id = sb("expert_id", [P, T, 2, E])
        minus_half = sb("minus_half", [P, T])
        base_e = sb("base_e", [P, T])
        low_rows = sb("low_rows", [P, 2])
        max_rows = sb("max_rows", [P, 2])
        pick = sb("pick", [2 * E, E, P], F32R)
        w1h, w1l = sb("w1h", [P, J * P], F32R), sb("w1l", [P, J * P], F32R)
        w2h, w2l = sb("w2h", [P, J * P], F32R), sb("w2l", [P, J * P], F32R)
        b1 = sb("b1", [P, J])
        b2 = sb("b2", [2 * E, D])
        wsh, wsl = sb("wsh", [P, 2, NG * P], F32R), sb("wsl", [P, 2, NG * P], F32R)
        wvh, wvl = sb("wvh", [P, D], F32R), sb("wvl", [P, D], F32R)
        wo = sb("wo", [P, D])
        wqkv = sb("wqkv", [P, 3 * D])
        wout = sb("wout", [P, D])
        wrh, wrl = sb("wrh", [P, E], F32R), sb("wrl", [P, E], F32R)
        bkv = sb("bkv", [P, 2 * D])
        bout = sb("bout", [P, D])
        lnw, lnb = sb("lnw", [P, D]), sb("lnb", [P, D])
        br = sb("br", [P, E])
        cols = sb("cols", [P, 3])

        x0, xa, nrm = sb("x0", [P, T, D]), sb("xa", [P, T, D]), sb("nrm", [P, T, D])
        x1, x2, x3 = sb("x1", [P, T, D]), sb("x2", [P, T, D]), sb("x3", [P, T, D])
        h = [sb("h1", [P, T, D]), sb("h3", [P, T, D])]
        z = sb("z", [P, T, D])
        hh = [sb("hh0", [P, L], F32R), sb("hh1", [P, L], F32R)]
        hl = [sb("hl0", [P, L], F32R), sb("hl1", [P, L], F32R)]
        xnT = sb("xnT", [P, L])
        qT = sb("qT", [P, L])
        kv = sb("kv", [P, T, 2 * D])
        sm = sb("sm", [P, P])
        smx = sb("smx", [P, 4])
        cwT = [sb("cwT0", [2 * E, L], F32R), sb("cwT1", [2 * E, L], F32R)]
        mix = sb("mix", [P, E, L])
        acc = sb("acc", [P, L])
        work = sb("work", [P, RP * PW])
        g32 = [work[:, k * L:(k + 1) * L] for k in range(RG)]
        weighted = [work[:, (RG + k) * L:(RG + k + 1) * L] for k in range(2)]
        parts = sb("parts", [P, 10 * L], F32R)
        gh = [parts[:, k * L:(k + 1) * L] for k in range(RG)]
        gl = [parts[:, (RG + k) * L:(RG + k + 1) * L] for k in range(RG)]
        stack = [[parts[:, (2 * g + s) * L:(2 * g + s + 1) * L] for s in range(2)] for g in range(NG)]
        stack_low = [parts[:, (8 + s) * L:(9 + s) * L] for s in range(2)]
        V = sb("V", [P, T, NH, HS])
        hmax = sb("hmax", [P, NG, 4, T])
        spread = sb("spread", [P, T, P])
        junk = sb("junk", [P, 2, L], BF16)
        oT = sb("oT", [P, L])
        inv = sb("inv", [P, T, 4])
        o = sb("o", [P, T, D])
        LNS = ["la", "lb", "l1", "l2", "l3", "z1", "z2"]
        ln = {k: (sb(f"{k}_st", [P, T, 6]), sb(f"{k}_mv", [P, T, 2]), sb(f"{k}_ve", [P, T]), sb(f"{k}_rs", [P, T]))
              for k in LNS}
        lg = sb("lg", [P, T, E])
        top = sb("top", [P, T, E])
        topi = sb("topi", [P, T, E], U32)
        topf = sb("topf", [P, T, 2])
        gap, ratio, one_more = sb("gap", [P, T]), sb("ratio", [P, T]), sb("one_more", [P, T])
        share = sb("share", [P, T, 2])
        chosen = sb("chosen", [P, T, 2, E])
        cw = sb("cw", [P, T, E])
        cwp = sb("cwp", [P, T, 2 * E])

        bank = [ctx.enter_context(nc.psum_tensor(f"bank{k}", [P, L], F32)) for k in range(8)]
        PV, MISC = bank[6], bank[7]

        LOADS = ["w1", "w2", "b1", "b2a", "b2b", "wk", "wq", "wv", "wo", "wqkv", "wout", "wr", "bkv", "bout",
                 "lnw", "br", "g", "b", "bq"]
        for k in LOADS:
            sem("ld_" + k, 16)
        sem("x_loaded", 16)
        sem("z_stored", 16)
        sem("pool_const", 1)
        sem("dve_const", 1)
        sem("w_high", 8)
        sem("w_low", 8)
        for k in LNS:
            sem(k + "_stats", T)
            sem(k + "_moments", T)
            sem(k + "_vareps", 1)
            sem(k + "_rstd", 1)
            sem(k + "_normed", T)
        sem("up_done", J)
        sem("gelu_done", J)
        sem("split_done", J)
        sem("down_done", J)
        sem("weighted_done", E)
        sem("summed", E - 1)
        for s in "12":
            sem(f"z{s}_back", 1)
            sem(f"z{s}_resid", 1)
            sem(f"z{s}_affine", 2)
            sem(f"x{2 * int(s) - 1}_biased", 1)
        for t in "123":
            sem(f"t{t}_turned", 1)
            sem(f"t{t}_high", 1)
            sem(f"t{t}_low", 1)
        for r in "12":
            sem(f"r{r}_logits", 1)
            sem(f"r{r}_pick", 10)
            sem(f"r{r}_ratio", 1)
            sem(f"r{r}_share", 9)
            sem(f"r{r}_turned", 1)
            sem(f"r{r}_cwT", 1)
            sem(f"r{r}_spread", E)
            sem(f"r{r}_mix_act", len(BY_ACT[int(r)]))
            sem(f"r{r}_mix_dve", len(BY_DVE[int(r)]))
        sem("x0_sums", 2)
        sem("xn_turned", 1)
        sem("xn_ready", 1)
        sem("kv_done", 2)
        sem("kv_biased", 2)
        sem("q_done", 1)
        sem("q_biased", 1)
        sem("ktv_done", 1)
        sem("ktv_max", 2)
        sem("ktv_exp", 1)
        sem("ktv_soft", 2)
        sem("lin_mixed", 1)
        sem("lin_copied", 1)
        sem("lin_out", 1)
        sem("x1_done", 1)
        sem("stack_mm", 2 * NG)
        sem("stack_low", 2 * NG)
        sem("stack_done", 2 * NG)
        sem("v_mm", 1)
        sem("v_done", 1)
        sem("logit_mm", 3 * NH)
        sem("max_done", 4 * NH)
        sem("max_spread", 2 * NG)
        sem("max_turned", NG)
        sem("max_in_q", NG)
        sem("pair_mm", 3 * NH)
        sem("exp_done", 3 * NH)
        sem("pv_done", NG)
        sem("pv_copied", NG)
        sem("pv_turned", NG)
        sem("inv_done", NG)
        sem("o_normed", NG)
        sem("o_turned", 1)
        sem("o_copied", 1)
        sem("wo_done", 1)
        sem("x3_done", 1)

        x_tiles = x.rearrange("b (t p) d -> b p t d", p=P)
        out_tiles = out.rearrange("b (t p) d -> b p t d", p=P)

        def every_iteration(eng, body):
            body(0, False, True)
            with eng.Fori(1, B - 1) as i:
                body(i, True, True)
            body(B - 1, True, False)
            body(B, True, False)

        made = {}
        W_PARTS = []
        for src, hi, lo in ((mix[:, :, :].rearrange("p e n -> p (e n)"), w1h, w1l), (work[:, 0:J * P], w2h, w2l)):
            for k in range(4):
                c = slice(k * J * P // 4, (k + 1) * J * P // 4)
                W_PARTS.append((src[:, c], hi[:, c], lo[:, c]))

        block = ctx.enter_context(nc.Block())

        @block.sync
        def _(sp):
            def load(name, dst, src):
                sp.dma_start(dst, src).then_inc(S["ld_" + name], 16)

            sp.dma_start(x0[:, :, :], x_tiles[0]).then_inc(S["x_loaded"], 16)
            load("wqkv", wqkv[:, :], w["wqkv"])
            load("g", cols[:, 0:1], w["g"])
            load("b", cols[:, 1:2], w["b"])
            load("bq", cols[:, 2:3], w["bqkv"][0:D].rearrange("(p a) -> p a", a=1))
            load("bkv", bkv[:, :], w["bqkv"][D:3 * D].partition_broadcast(P))
            load("bout", bout[:, :], w["bout"].partition_broadcast(P))
            load("wout", wout[:, :], w["wout"])
            load("wr", lg[:, 0, :], w["wr"])
            load("br", br[:, :], w["br"].partition_broadcast(P))
            sp.dma_start(lnb[:, :], w["lnb"].partition_broadcast(P)).then_inc(S["z_stored"], 16)
            load("w1", mix[:, :, :], w["w1"].rearrange("p (e n) -> p e n", e=E))
            load("w2", work[:, 0:J * P], w["w2"])
            load("b1", b1[:, :], w["b1"])
            load("b2a", b2[0:E, :], w["b2"])
            load("b2b", b2[E:2 * E, :], w["b2"])
            load("wk", x2[:, 0, :], w["wk"])
            load("wq", x2[:, 1, :], w["wq"])
            load("wv", x2[:, 2, :], w["wv"])
            load("wo", wo[:, :], w["wo"])
            load("lnw", lnw[:, :], w["lnw"].partition_broadcast(P))

            def body(i, second, more):
                if more:
                    sp.wait_ge(S["x1_done"], at("x1_done", i, 1))
                    sp.dma_start(x0[:, :, :], x_tiles[i + 1]).then_inc(S["x_loaded"], 16)
                if second:
                    sp.wait_ge(S["z2_affine"], at("z2_affine", i - 1, 2))
                    sp.dma_start(out_tiles[i - 1], z[:, :, :]).then_inc(S["z_stored"], 16)

            every_iteration(sp, body)
            sp.wait_ge(S["z_stored"], at("z_stored", B, 16))

        @block.gpsimd
        def _(gp):
            consts = [0]

            def const(ins):
                ins.then_inc(S["pool_const"], 1)
                consts[0] += 1
                gp.wait_ge(S["pool_const"], consts[0])

            def keep(ap, op, fill, base, pattern, mult):
                const(nc.gpsimd.affine_select(out=ap, in_=ap, compare_op=op, fill=fill, base=base,
                                              pattern=pattern, channel_multiplier=mult))

            def rstd(k, n, eps):
                st, mv, ve, rs = ln[k]
                gp.wait_ge(S[k + "_moments"], at(k + "_moments", n, T))
                settle(gp)
                nc.gpsimd.tensor_scalar(ve[:, :], mv[:, :, 1], eps, None, ALU.add).then_inc(S[k + "_vareps"], 1)
                gp.wait_ge(S[k + "_vareps"], at(k + "_vareps", n, 1))
                nc.gpsimd.tensor_tensor(rs[:, :], ve[:, :], minus_half[:, :], ALU.pow).then_inc(S[k + "_rstd"], 1)

            def router(r, n):
                gp.wait_ge(S[f"r{r}_pick"], at(f"r{r}_pick", n, 10))
                nc.gpsimd.tensor_tensor(ratio[:, :], base_e[:, :], gap[:, :], ALU.pow).then_inc(S[f"r{r}_ratio"], 1)

            def moe_sum(n, e):
                gp.wait_ge(S["weighted_done"], at("weighted_done", n, e + 1))
                if e > 1:
                    gp.wait_ge(S["summed"], at("summed", n, e - 1))
                nc.gpsimd.tensor_tensor(acc[:, :], acc[:, :], weighted[e % 2], ALU.add).then_inc(S["summed"], 1)

            def bias_x(s, xt, n):
                k = ("l1", "l3")[s]
                gp.wait_ge(S[k + "_normed"], at(k + "_normed", n, T))
                nc.gpsimd.tensor_tensor(xt[:, :, :], xt[:, :, :], lnb[:, None, :].to_broadcast([P, T, D]),
                                        ALU.add).then_inc(S[f"x{2 * s + 1}_biased"], 1)

            def affine(s, n, xin, dst):
                gp.wait_ge(S[f"z{s}_normed"], at(f"z{s}_normed", n, T))
                nc.gpsimd.tensor_tensor(z[:, :, :], z[:, :, :], lnw[:, None, :].to_broadcast([P, T, D]),
                                        ALU.mult).then_inc(S[f"z{s}_affine"], 1)
                gp.wait_ge(S[f"z{s}_affine"], at(f"z{s}_affine", n, 1))
                gp.wait_ge(S[f"x{2 * s - 1}_biased"], at(f"x{2 * s - 1}_biased", n, 1))
                nc.gpsimd.tensor_tensor(dst[:, :, :], z[:, :, :], xin[:, :, :], ALU.add).then_inc(S[f"z{s}_affine"], 1)

            def x0_plus_xa(n):
                gp.wait_ge(S["la_normed"], at("la_normed", n, T))
                nc.gpsimd.tensor_tensor(x0[:, :, :], x0[:, :, :], xa[:, :, :], ALU.add).then_inc(S["x0_sums"], 1)

            def x0_plus_bias(n):
                gp.wait_ge(S["x0_sums"], at("x0_sums", n, 1))
                nc.gpsimd.tensor_tensor(x0[:, :, :], x0[:, :, :], bout[:, None, :].to_broadcast([P, T, D]),
                                        ALU.add).then_inc(S["x0_sums"], 1)

            const(nc.gpsimd.memset(minus_half[:, :], -0.5))
            const(nc.gpsimd.memset(base_e[:, :], 2.718281828459045))
            const(nc.gpsimd.memset(ident[:, :], 0.0))
            keep(ident[:, :], ALU.not_equal, 1.0, 0, [[-1, P]], 1)
            made["ident"] = consts[0]
            rstd("la", 0, 1e-5)
            gp.wait_ge(S["ld_bout"], 16)
            x0_plus_xa(0)
            rstd("lb", 0, 1e-5)
            x0_plus_bias(0)
            const(nc.gpsimd.memset(head_mask[:, :], 0.0))
            hm = head_mask[:, :].rearrange("p (h e) -> p h e", e=HD)
            keep(hm, ALU.is_ge, NEG, 0, [[-HD, NH], [0, HD]], 1)
            keep(hm, ALU.is_ge, NEG, HD - 1, [[HD, NH], [0, HD]], -1)
            made["head_mask"] = consts[0]
            for half in range(2):
                pv = (x3, o)[half][0:2 * E, :, :]
                const(nc.gpsimd.memset(pv, 0.0))
                for r in range(2):
                    keep(pv, ALU.not_equal, 1.0, -(half * E // 2 + r * E), [[-1, E // 2], [0, P]], 1)
            made["pick"] = consts[0]
            const(nc.gpsimd.iota(expert_id[:, :, :, :], [[0, T], [0, 2], [1, E]], base=0, channel_multiplier=0,
                                 allow_small_or_imprecise_dtypes=True))
            made["expert_id"] = consts[0]
            rstd("l1", 0, 1e-5)
            gp.wait_ge(S["z_stored"], at("z_stored", 0, 16))
            bias_x(0, x1, 0)
            router(1, 0)
            const(nc.gpsimd.memset(causal[:, :], 0.0))
            keep(causal[:, L - P:L], ALU.is_ge, NEG, 0, [[-1, P]], 1)
            const(nc.gpsimd.memset(ident_b[:, :], 0.0))
            keep(ident_b[:, :], ALU.not_equal, 1.0, 0, [[-1, P]], 1)
            const(nc.gpsimd.memset(later[:, :], 0.0))
            keep(later[:, :], ALU.is_ge, NEG, 0, [[1, P]], -1)
            const(nc.gpsimd.memset(h[1][:, :, :], 0.0))
            for k, (lo, hi) in enumerate(((HD, 2 * HD), (2 * HD, 3 * HD), (3 * HD, 3 * HD + 2))):
                const(nc.gpsimd.memset(h[1][:, k, :].rearrange("p (j r) -> p j r", r=HS)[:, :, lo:hi], 1.0))
            const(nc.gpsimd.memset(V[:, :, :, :], 0.0))
            const(nc.gpsimd.memset(V[:, :, :, HD:HD + 1], 1.0))
            const(nc.gpsimd.memset(spread[:, :, :], 0.0))
            made["all"] = consts[0]
            gp.wait_ge(S["ld_lnw"], 16)

            def body(i, second, more):
                last = isinstance(i, int) and i == B
                if last:
                    rstd("l3", i - 1, 1e-5)
                    bias_x(1, x3, i - 1)
                    router(2, i - 1)
                else:
                    for e in range(1, E):
                        if second:
                            if e == 2:
                                rstd("l3", i - 1, 1e-5)
                            if e == 3:
                                bias_x(1, x3, i - 1)
                            if e == 5:
                                router(2, i - 1)
                            if e == 6 and more:
                                rstd("la", i + 1, 1e-5)
                            if e == 7 and more:
                                x0_plus_xa(i + 1)
                        elif e == 1:
                            rstd("la", i + 1, 1e-5)
                            x0_plus_xa(i + 1)
                            rstd("lb", i + 1, 1e-5)
                            x0_plus_bias(i + 1)
                        moe_sum(2 * i - 1 if second else 0, e)
                if second:
                    for e in range(1, E):
                        if not last:
                            if e == 1:
                                if more:
                                    rstd("lb", i + 1, 1e-5)
                                    x0_plus_bias(i + 1)
                                rstd("z1", i, 1e-12)
                                affine(1, i, x1, x2)
                                rstd("l2", i, 1e-5)
                        moe_sum(2 * i - 1 if last else 2 * i, e)
                else:
                    rstd("z1", i, 1e-12)
                    affine(1, i, x1, x2)
                    rstd("l2", i, 1e-5)
                if second:
                    rstd("z2", i - 1, 1e-12)
                if more:
                    rstd("l1", i + 1, 1e-5)
                if second:
                    affine(2, i - 1, x3, z)
                if more:
                    bias_x(0, x1, i + 1)
                    router(1, i + 1)

            every_iteration(gp, body)

        @block.scalar
        def _(ac):
            def act(out_, in_, fn, name, **kw):
                return nc.scalar.activation(out_, in_, fn, **kw).then_inc(S[name], 1)

            def high_part(t, slot, n):
                ac.wait_ge(S[f"t{t}_turned"], at(f"t{t}_turned", n, 1))
                act(hh[slot][:, :], MISC[:, :], ACT.Copy, f"t{t}_high")

            def router(r, n):
                ac.wait_ge(S[f"r{r}_turned"], at(f"r{r}_turned", n, 1))
                act(cwT[r - 1][:, :], MISC[0:2 * E, :], ACT.Copy, f"r{r}_cwT")

            def mix_copy(r, n, e, src, nmoe=None):
                assert mix_done(r, e)[0] == f"r{r}_mix_act"
                ac.wait_ge(S[f"r{r}_spread"], at(f"r{r}_spread", n, e + 1))
                if nmoe is not None:
                    ac.wait_ge(S["weighted_done"], at("weighted_done", nmoe, e + 1))
                act(mix[:, e, :], src[:, :], ACT.Copy, f"r{r}_mix_act")

            def moe_gelu(n, j):
                ac.wait_ge(S["up_done"], at("up_done", n, j + 1))
                wait(ac, "split_done", n, j - RG + 1)
                nc.scalar.activation(g32[j % RG], bank[j % 4][:, :], ACT.Gelu, bias=b1[:, j:j + 1])
                wait(ac, "down_done", n, j - RG + 1)
                act(gh[j % RG], bank[j % 4][:, :], ACT.Gelu, "gelu_done", bias=b1[:, j:j + 1])

            def moe(n, beside):
                for j in range(J):
                    moe_gelu(n, j)
                    beside(j)

            def linear_1a(n, src):
                ac.wait_ge(S["xn_turned"], at("xn_turned", n, 1))
                act(xnT[:, :], src[:, :], ACT.Identity, "xn_ready", scale=cols[:, 0:1], bias=cols[:, 1:2])

            def linear_1b(n, src):
                ac.wait_ge(S["q_done"], at("q_done", n, 1))
                act(qT[:, :], src[:, :], ACT.Identity, "q_biased", bias=cols[:, 2:3])

            def linear_2a(n):
                ac.wait_ge(S["ktv_max"], at("ktv_max", n, 2))
                act(sm[:, :], sm[:, :], ACT.Exp, "ktv_exp", bias=smx[:, 0:1], accum_out=smx[:, 1:2])

            def linear_2b(n):
                ac.wait_ge(S["lin_mixed"], at("lin_mixed", n, 1))
                act(xnT[:, :], MISC[:, :], ACT.Copy, "lin_copied")

            def pv_copy(i, g):
                ac.wait_ge(S["pv_done"], at("pv_done", i, g + 1))
                wait(ac, "pv_turned", i, g)
                act(oT[:, :], PV[:, :], ACT.Copy, "pv_copied")

            def o_copy(i):
                ac.wait_ge(S["o_turned"], at("o_turned", i, 1))
                act(oT[:, :], MISC[:, :], ACT.Copy, "o_copied")

            for k in ("g", "b", "bq"):
                ac.wait_ge(S["ld_" + k], 16)

            def weight_high(k):
                if k == 0:
                    ac.wait_ge(S["ld_w1"], 16)
                if k == 4:
                    ac.wait_ge(S["ld_w2"], 16)
                src, hi, _ = W_PARTS[k]
                act(hi, src, ACT.Copy, "w_high")

            linear_1a(0, PV)
            weight_high(0)
            weight_high(1)
            linear_1b(0, PV)
            weight_high(2)
            weight_high(3)
            linear_2a(0)
            weight_high(4)
            linear_2b(0)
            weight_high(5)
            weight_high(6)
            weight_high(7)
            high_part(1, 0, 0)
            router(1, 0)
            ac.wait_ge(S["w_low"], 4)
            mix_copy(1, 0, 0, MISC)
            ac.wait_ge(S["ld_b1"], 16)
            ac.wait_ge(S["w_low"], 8)

            def body(i, second, more):
                last = isinstance(i, int) and i == B

                def beside_1(j):
                    if not second:
                        if j == 13:
                            linear_1a(i + 1, MISC)
                        if j == 25:
                            linear_1b(i + 1, MISC)
                        return
                    if j == 7:
                        o_copy(i - 1)
                    if j == 17:
                        high_part(3, 1, i - 1)
                    if j == 28:
                        router(2, i - 1)

                def beside_2(j):
                    n1 = None if last else 2 * i - 1
                    if j == 0 and not last:
                        mix_copy(2, i - 1, 0, MISC, n1)
                    if j == 4:
                        mix_copy(2, i - 1, 2, PV, n1)
                    if j == 12:
                        mix_copy(2, i - 1, 5, MISC, n1)
                    if j == 16 and not last:
                        high_part(2, 0, i)
                    if j == 20:
                        mix_copy(2, i - 1, 6, MISC, n1)
                    if more:
                        if j == 11:
                            linear_1a(i + 1, PV)
                        if j == 23:
                            linear_1b(i + 1, PV)

                if not last:
                    moe(2 * i - 1 if second else 0, beside_1)
                else:
                    o_copy(i - 1)
                    high_part(3, 1, i - 1)
                    router(2, i - 1)
                    mix_copy(2, i - 1, 0, MISC)
                if second:
                    moe(2 * i - 1 if last else 2 * i, beside_2)
                    if last:
                        return
                else:
                    high_part(2, 0, i)
                if more:
                    linear_2a(i + 1)
                for u in range(2 * NG):
                    g, s = u // 2, u % 2
                    ac.wait_ge(S["stack_mm"], at("stack_mm", i, u + 1))
                    wait(ac, "stack_done", i, u - 1)
                    act(stack_low[u % 2], bank[u % 6][:, :], ACT.Copy, "stack_low", scale=low_rows[:, s:s + 1])
                ac.wait_ge(S["v_mm"], at("v_mm", i, 1))
                act(V[:, :, :, 0:HD], MISC[:, :].rearrange("p (t h d) -> p t h d", t=T, d=HD), ACT.Copy, "v_done")
                for s in range(NH + LAG):
                    if s >= LAG:
                        hd = s - LAG
                        if hd >= RP:
                            ac.wait_ge(S["pv_done"], at("pv_done", i, (hd - RP) // 4 + 1))
                        pr = work[:, (hd % RP) * PW:(hd % RP + 1) * PW]
                        for u, (lo, hi) in enumerate(((0, 512), (512, 1024), (1024, 1280))):
                            ac.wait_ge(S["pair_mm"], at("pair_mm", i, 3 * hd + u + 1))
                            act(pr[:, lo:hi], bank[3 + u][:, 0:hi - lo], ACT.Exp, "exp_done", scale=SCALE)
                    if more:
                        if s == 1:
                            linear_2b(i + 1)
                        if s == 6:
                            high_part(1, 0, i + 1)
                        if s == 12:
                            router(1, i + 1)
                        if s == 14:
                            mix_copy(1, i + 1, 0, MISC)
                    if s >= LAG + 5 and (s - LAG - 5) % 4 == 0:
                        pv_copy(i, (s - LAG - 5) // 4)
                pv_copy(i, NG - 1)

            every_iteration(ac, body)

        @block.vector
        def _(ve):
            def stats(k, src, n, ready=None):
                st, mv, _, _ = ln[k]
                for t in range(T):
                    if ready is not None:
                        ready(t)
                    nc.vector.bn_stats(st[:, t, :], src[:, t, :]).then_inc(S[k + "_stats"], 1)
                ve.wait_ge(S[k + "_stats"], at(k + "_stats", n, T))
                settle(ve)
                for t in range(T):
                    nc.vector.bn_aggr(mv[:, t, :], st[:, t, :]).then_inc(S[k + "_moments"], 1)

            def norm(k, dst, src, n):
                st, mv, _, rs = ln[k]
                ve.wait_ge(S[k + "_rstd"], at(k + "_rstd", n, 1))
                for t in range(T):
                    nc.vector.tensor_scalar(dst[:, t, :], src[:, t, :], mv[:, t, 0:1], rs[:, t:t + 1],
                                            ALU.subtract, ALU.mult).then_inc(S[k + "_normed"], 1)

            consts = [0]

            def const(ins):
                ins.then_inc(S["dve_const"], 1)
                consts[0] += 1

            def settled():
                ve.wait_ge(S["dve_const"], consts[0])

            def split(hi, lo, src):
                const(nc.vector.tensor_copy(hi, src))
                settled()
                const(nc.vector.tensor_tensor(lo, src, hi.bitcast(F32), ALU.subtract))

            def weight_low(k):
                src, hi, lo = W_PARTS[k]
                ve.wait_ge(S["w_high"], k + 1)
                nc.vector.tensor_tensor(lo, src, hi.bitcast(F32), ALU.subtract).then_inc(S["w_low"], 1)

            def low_part(t, slot, n):
                ve.wait_ge(S[f"t{t}_high"], at(f"t{t}_high", n, 1))
                nc.vector.tensor_tensor(hl[slot][:, :], MISC[:, :], hh[slot][:, :].bitcast(F32),
                                        ALU.subtract).then_inc(S[f"t{t}_low"], 1)

            def router_1(r, n):
                k = f"r{r}_pick"
                ve.wait_ge(S[f"r{r}_logits"], at(f"r{r}_logits", n, 1))
                nc.vector.tensor_tensor(lg[:, :, :], MISC[:, 0:T * E].rearrange("p (t e) -> p t e", e=E),
                                        br[:, None, :].to_broadcast([P, T, E]), ALU.add).then_inc(S[k], 1)
                ve.wait_ge(S[k], at(k, n, 1))
                settle(ve)
                for t in range(T):
                    nc.vector.max(top[:, t, :], lg[:, t, :]).then_inc(S[k], 1)
                ve.wait_ge(S[k], at(k, n, 5))
                nc.vector.tensor_tensor(gap[:, :], top[:, :, 1], top[:, :, 0], ALU.subtract).then_inc(S[k], 1)
                for t in range(T):
                    nc.vector.max_index(topi[:, t, :], top[:, t, :], lg[:, t, :]).then_inc(S[k], 1)

            def router_2(r, n):
                k = f"r{r}_share"
                ve.wait_ge(S[f"r{r}_pick"], at(f"r{r}_pick", n, 10))
                nc.vector.tensor_copy(topf[:, :, :], topi[:, :, 0:2]).then_inc(S[k], 1)
                ve.wait_ge(S[f"r{r}_ratio"], at(f"r{r}_ratio", n, 1))
                nc.vector.tensor_scalar(one_more[:, :], ratio[:, :], 1.0, None, ALU.add).then_inc(S[k], 1)
                ve.wait_ge(S[k], at(k, n, 2))
                nc.vector.reciprocal(share[:, :, 0], one_more[:, :]).then_inc(S[k], 1)
                nc.vector.tensor_tensor(chosen[:, :, :, :], expert_id[:, :, :, :],
                                        topf[:, :, :, None].to_broadcast([P, T, 2, E]),
                                        ALU.is_equal).then_inc(S[k], 1)
                ve.wait_ge(S[k], at(k, n, 4))
                nc.vector.tensor_tensor(share[:, :, 1], share[:, :, 0], ratio[:, :], ALU.mult).then_inc(S[k], 1)
                ve.wait_ge(S[k], at(k, n, 5))
                nc.vector.tensor_tensor(chosen[:, :, :, :], chosen[:, :, :, :],
                                        share[:, :, :, None].to_broadcast([P, T, 2, E]),
                                        ALU.mult).then_inc(S[k], 1)
                ve.wait_ge(S[k], at(k, n, 6))
                nc.vector.tensor_tensor(cw[:, :, :], chosen[:, :, 0, :], chosen[:, :, 1, :], ALU.add).then_inc(S[k], 1)
                ve.wait_ge(S[k], at(k, n, 7))
                nc.vector.tensor_copy(cwp[:, :, 0:E].bitcast(F32R), cw[:, :, :]).then_inc(S[k], 1)
                ve.wait_ge(S[k], at(k, n, 8))
                nc.vector.tensor_tensor(cwp[:, :, E:2 * E], cw[:, :, :], cwp[:, :, 0:E], ALU.subtract).then_inc(S[k], 1)

            def moe_split(n, j):
                ve.wait_ge(S["gelu_done"], at("gelu_done", n, j + 1))
                wait(ve, "down_done", n, j - RG + 1)
                nc.vector.tensor_tensor(gl[j % RG], g32[j % RG], gh[j % RG].bitcast(F32),
                                        ALU.subtract).then_inc(S["split_done"], 1)

            def mix_copy(r, n, e, src, nmoe=None):
                assert mix_done(r, e)[0] == f"r{r}_mix_dve"
                ve.wait_ge(S[f"r{r}_spread"], at(f"r{r}_spread", n, e + 1))
                if nmoe is not None:
                    ve.wait_ge(S["weighted_done"], at("weighted_done", nmoe, e + 1))
                nc.vector.tensor_copy(mix[:, e, :], src[:, :]).then_inc(S[f"r{r}_mix_dve"], 1)

            def moe_weigh(n, e, r, nb, acc_read):
                name, k = mix_done(r, e)
                ve.wait_ge(S["down_done"], at("down_done", n, FT * e + FT))
                ve.wait_ge(S[name], at(name, nb, k))
                if e == 0 and acc_read is not None:
                    wait(ve, *acc_read)
                if e >= 2:
                    wait(ve, "summed", n, e - 2)
                nc.vector.tensor_tensor(acc[:, :] if e == 0 else weighted[e % 2], bank[4 + e % 2][:, :],
                                        mix[:, e, :], ALU.mult).then_inc(S["weighted_done"], 1)

            def moe(n, r, nb, beside, acc_read=None):
                for j in range(J):
                    moe_split(n, j)
                    if j >= 5 and (j - 5) % FT == 0:
                        moe_weigh(n, (j - 5) // FT, r, nb, acc_read)
                    beside(j)
                moe_weigh(n, E - 1, r, nb, None)

            def end_moe(s, n, z_free):
                ve.wait_ge(S[f"z{s}_back"], at(f"z{s}_back", n, 1))
                wait(ve, *z_free)
                nc.vector.tensor_tensor(z[:, :, :], MISC[:, :].rearrange("p (t d) -> p t d", t=T), h[s - 1][:, :, :],
                                        ALU.add).then_inc(S[f"z{s}_resid"], 1)

            def z_stats(s, n):
                ve.wait_ge(S[f"z{s}_resid"], at(f"z{s}_resid", n, 1))
                stats(f"z{s}", z, n)

            def linear_a(n):
                ve.wait_ge(S["x_loaded"], at("x_loaded", n, 16))
                stats("la", x0, n)

            def linear_b(n):
                stats("lb", xa, n, lambda t: wait(ve, "la_normed", n, t + 1))

            def linear_kv(n, c, src):
                ve.wait_ge(S["kv_done"], at("kv_done", n, c + 1))
                nc.vector.tensor_tensor(kv[:, 2 * c:2 * c + 2, :], src[:, :].rearrange("p (t d) -> p t d", t=2),
                                        bkv[:, None, :].to_broadcast([P, 2, 2 * D]), ALU.add).then_inc(S["kv_biased"], 1)

            def linear_max(n, src):
                ve.wait_ge(S["ktv_done"], at("ktv_done", n, 1))
                nc.vector.tensor_tensor(sm[:, :], src[:, 0:P], head_mask[:, :], ALU.add).then_inc(S["ktv_max"], 1)
                ve.wait_ge(S["ktv_max"], at("ktv_max", n, 1))
                nc.vector.tensor_reduce(smx[:, 0:1], sm[:, :], AX.X, ALU.max, negate=True).then_inc(S["ktv_max"], 1)

            def linear_2a(n):
                ve.wait_ge(S["ktv_exp"], at("ktv_exp", n, 1))
                nc.vector.reciprocal(smx[:, 2:3], smx[:, 1:2]).then_inc(S["ktv_soft"], 1)
                ve.wait_ge(S["ktv_soft"], at("ktv_soft", n, 1))
                nc.vector.tensor_scalar(sm[:, :], sm[:, :], smx[:, 2:3], None, ALU.mult).then_inc(S["ktv_soft"], 1)

            def linear_2b(n):
                ve.wait_ge(S["lin_out"], at("lin_out", n, 1))
                ve.wait_ge(S["x0_sums"], at("x0_sums", n, 2))
                nc.vector.tensor_tensor(x1[:, :, :], MISC[:, :].rearrange("p (t d) -> p t d", t=T), x0[:, :, :],
                                        ALU.add).then_inc(S["x1_done"], 1)

            linear_a(0)
            norm("la", xa, x0, 0)
            for k in ("bkv", "wr", "br"):
                ve.wait_ge(S["ld_" + k], 16)
            split(wrh[:, :], wrl[:, :], lg[:, 0, :])
            settled()
            made["wr"] = consts[0]
            linear_b(0)
            norm("lb", nrm, xa, 0)
            linear_kv(0, 0, PV)
            linear_kv(0, 1, MISC)
            weight_low(0)
            ve.wait_ge(S["pool_const"], made["head_mask"])
            linear_max(0, MISC)
            weight_low(1)
            linear_2a(0)
            weight_low(2)
            weight_low(3)
            linear_2b(0)
            ve.wait_ge(S["x1_done"], at("x1_done", 0, 1))
            stats("l1", x1, 0)
            weight_low(4)
            norm("l1", h[0], x1, 0)
            ve.wait_ge(S["pool_const"], made["pick"])
            for half in range(2):
                const(nc.vector.tensor_copy(pick[:, half * E // 2:(half + 1) * E // 2, :], (x3, o)[half][0:2 * E, :, :]))
            made["pick_r"] = consts[0]
            low_part(1, 0, 0)
            router_1(1, 0)
            weight_low(5)
            weight_low(6)
            ve.wait_ge(S["pool_const"], made["expert_id"])
            router_2(1, 0)
            weight_low(7)
            ve.wait_ge(S["w_low"], 4)
            mix_copy(1, 0, 1, PV)

            def row_masks():
                ve.wait_ge(S["pool_const"], made["all"])
                const(nc.vector.memset(max_rows[:, :], 0.0))
                const(nc.vector.tensor_tensor(z[:, 0:3, :], h[1][:, 0:3, :],
                                              ident[:, None, :].to_broadcast([P, 3, P]), ALU.mult))
                settled()
                const(nc.vector.tensor_reduce(low_rows[:, :], z[:, 0:2, :], AX.X, ALU.add))
                const(nc.vector.tensor_reduce(max_rows[:, 0:1], z[:, 2, :], AX.X, ALU.add))

            def stack_weights(s):
                for k in ("wk", "wq", "wv"):
                    ve.wait_ge(S["ld_" + k], 16)
                dst = x3[:, :, :].rearrange("p t (g r) -> p (t g) r", r=HS)
                src = x2[:, s, :].rearrange("p (h d) -> p h d", d=HD)
                settled()
                const(nc.vector.memset(x3[:, :, :], 0.0))
                settled()
                for r in range(3):
                    const(nc.vector.tensor_copy(dst[:, :, r * HD:(r + 1) * HD], src))
                settled()
                split(wsh[:, s, :], wsl[:, s, :], x3[:, :, :].rearrange("p t n -> p (t n)"))

            def body(i, second, more):
                last = isinstance(i, int) and i == B

                def beside_1(j):
                    if j in (3, 7, 11, 15, 19, 23):
                        mix_copy(1, i, 2 + j // 4, PV)
                    if second and more:
                        if j == 28:
                            linear_a(i + 1)
                        if j == 30:
                            norm("la", xa, x0, i + 1)
                    if not second:
                        if j == 2:
                            linear_a(i + 1)
                        if j == 4:
                            norm("la", xa, x0, i + 1)
                        if j == 6:
                            linear_b(i + 1)
                        if j == 8:
                            norm("lb", nrm, xa, i + 1)
                        if j in (17, 21):
                            linear_kv(i + 1, (j - 17) // 4, MISC)
                        if j == 29:
                            linear_max(i + 1, MISC)
                        if j == 24:
                            row_masks()
                        if j in (26, 28):
                            stack_weights((j - 26) // 2)
                        if j == 30:
                            split(wvh[:, :], wvl[:, :], x2[:, 2, :])
                            settled()
                            made["stacks"] = consts[0]
                        return
                    if j == 3:
                        normalize(i - 1, NG - 1)
                    if j == 11:
                        x3_sum(i - 1, ("x1_biased", i, 1))
                    if j == 13:
                        norm("l3", h[1], x3, i - 1)
                    if j == 18:
                        low_part(3, 1, i - 1)
                    if j == 22:
                        router_1(2, i - 1)
                    if j == 24:
                        router_2(2, i - 1)

                def beside_2(j):
                    n1 = None if last else 2 * i - 1
                    if j == 0 and not last:
                        mix_copy(2, i - 1, 1, PV, n1)
                    if j == 7:
                        mix_copy(2, i - 1, 3, PV, n1)
                    if j == 8:
                        mix_copy(2, i - 1, 4, MISC, n1)
                    if j == 24:
                        mix_copy(2, i - 1, 7, MISC, n1)
                    if last:
                        return
                    if j == 4:
                        end_moe(1, i, ("z_stored", i, 0))
                        z_stats(1, i)
                    if j == 6:
                        norm("z1", z, z, i)
                    if j == 9:
                        ve.wait_ge(S["z1_affine"], at("z1_affine", i, 2))
                        stats("l2", x2, i)
                    if j == 11:
                        wait(ve, "xn_turned", i + 1 if more else i, 1)
                        norm("l2", nrm, x2, i)
                    if j == 17:
                        low_part(2, 0, i)
                    if more:
                        if j == 1:
                            linear_b(i + 1)
                        if j == 3:
                            ve.wait_ge(S["t2_turned"], at("t2_turned", i - 1, 1))
                            norm("lb", nrm, xa, i + 1)
                        if j in (15, 19):
                            linear_kv(i + 1, (j - 15) // 4, PV)
                        if j == 27:
                            linear_max(i + 1, PV)

                if not last:
                    moe(2 * i - 1 if second else 0, 1, i, beside_1)
                else:
                    normalize(i - 1, NG - 1)
                    x3_sum(i - 1, ("z2_affine", i - 2, 2))
                    norm("l3", h[1], x3, i - 1)
                    low_part(3, 1, i - 1)
                    router_1(2, i - 1)
                    router_2(2, i - 1)
                    mix_copy(2, i - 1, 1, PV)
                if second:
                    moe(2 * i - 1 if last else 2 * i, 2, i - 1, beside_2,
                        None if last else ("z1_back", i, 1))
                else:
                    end_moe(1, i, ("z_stored", i, 0))
                    z_stats(1, i)
                    norm("z1", z, z, i)
                    ve.wait_ge(S["z1_affine"], at("z1_affine", i, 2))
                    stats("l2", x2, i)
                    ve.wait_ge(S["xn_turned"], at("xn_turned", i + 1, 1))
                    norm("l2", nrm, x2, i)
                    low_part(2, 0, i)
                if last:
                    end_moe(2, i - 1, ("z_stored", i - 1, 16))
                    z_stats(2, i - 1)
                    norm("z2", z, z, i - 1)
                    return
                if more:
                    linear_2a(i + 1)
                for u in range(2 * NG):
                    g, s = u // 2, u % 2
                    ve.wait_ge(S["stack_low"], at("stack_low", i, u + 1))
                    nc.vector.scalar_tensor_tensor(
                        out=stack[g][s], in0=bank[u % 6][:, :], scalar=max_rows[:, s:s + 1],
                        in1=stack_low[u % 2].bitcast(F32), op0=ALU.add, op1=ALU.subtract,
                    ).then_inc(S["stack_done"], 1)
                for s in range(NH + LAG):
                    if s < NH:
                        g, j = s // 4, s % 4
                        for k, qt in enumerate((3, 2, 0, 1)):
                            b_, c = Q_BANK[qt]
                            n_ = (qt + 1) * P
                            ve.wait_ge(S["logit_mm"], at("logit_mm", i, 3 * s + b_ + 1))
                            wait(ve, "max_done", i, 4 * s + k - 1)
                            settle(ve)
                            nc.vector.tensor_tensor_reduce(
                                junk[:, k % 2, 0:n_], bank[b_][:, c:c + n_], causal[:, L - n_:L], 1.0, NEG,
                                ALU.add, ALU.max, hmax[:, g, j, qt:qt + 1]).then_inc(S["max_done"], 1)
                        if j == 3:
                            src = hmax[:, g, :, :].rearrange("p j t -> p t j")
                            dst = spread[:, :, :].rearrange("p t (j r) -> p t j r", r=HS)
                            ve.wait_ge(S["max_done"], at("max_done", i, 4 * s + 4))
                            wait(ve, "max_turned", i, g)
                            nc.vector.tensor_copy(dst[:, :, :, 3 * HD].bitcast(F32R), src).then_inc(S["max_spread"], 1)
                            ve.wait_ge(S["max_spread"], at("max_spread", i, 2 * g + 1))
                            nc.vector.tensor_tensor(dst[:, :, :, 3 * HD + 1], src, dst[:, :, :, 3 * HD],
                                                    ALU.subtract).then_inc(S["max_spread"], 1)
                    if s in (5, 9, 13, 17):
                        g = (s - 5) // 4
                        ve.wait_ge(S["max_turned"], at("max_turned", i, g + 1))
                        nc.vector.tensor_tensor(stack[g][1], stack[g][1].bitcast(F32), MISC[:, :],
                                                ALU.subtract).then_inc(S["max_in_q"], 1)
                    if second:
                        if s == 0:
                            end_moe(2, i - 1, ("z1_affine", i, 2))
                        if s == 1:
                            z_stats(2, i - 1)
                        if s == 3:
                            norm("z2", z, z, i - 1)
                    if more:
                        if s == 2:
                            linear_2b(i + 1)
                        if s == 3:
                            ve.wait_ge(S["x1_done"], at("x1_done", i + 1, 1))
                            stats("l1", x1, i + 1)
                        if s == 5:
                            norm("l1", h[0], x1, i + 1)
                        if s == 7:
                            low_part(1, 0, i + 1)
                        if s == 8:
                            router_1(1, i + 1)
                        if s == 10:
                            router_2(1, i + 1)
                        if s == 15:
                            mix_copy(1, i + 1, 1, MISC)
                    if s in (12, 16, 20):
                        normalize(i, (s - 12) // 4)

            def x3_sum(i, x3_free):
                ve.wait_ge(S["wo_done"], at("wo_done", i, 1))
                wait(ve, *x3_free)
                nc.vector.tensor_tensor(x3[:, :, :], MISC[:, :].rearrange("p (t d) -> p t d", t=T), x2[:, :, :],
                                        ALU.add).then_inc(S["x3_done"], 1)
                ve.wait_ge(S["x3_done"], at("x3_done", i, 1))
                stats("l3", x3, i)

            def normalize(i, g):
                ve.wait_ge(S["pv_turned"], at("pv_turned", i, g + 1))
                wait(ve, "o_normed", i, g)
                src = MISC[:, :].rearrange("p (t j r) -> p t j r", t=T, r=HS)
                nc.vector.reciprocal(inv[:, :, :], src[:, :, :, HD]).then_inc(S["inv_done"], 1)
                ve.wait_ge(S["inv_done"], at("inv_done", i, g + 1))
                nc.vector.tensor_tensor(
                    o[:, :, :].rearrange("p t (g j d) -> p t g j d", g=NG, d=HD)[:, :, g], src[:, :, :, 0:HD],
                    inv[:, :, :, None].to_broadcast([P, T, 4, HD]), ALU.mult).then_inc(S["o_normed"], 1)

            every_iteration(ve, body)

        @block.tensor
        def _(pe):
            BANKS = {"MISC": MISC, "PV": PV}
            read_by = {}

            def misc_free(reader, which="MISC"):
                if which in read_by:
                    wait(pe, *read_by[which])
                read_by[which] = reader

            def turn(src, ready, name, n, reader, which="MISC"):
                misc_free(reader, which)
                for t in range(T):
                    ready(t)
                    ins = nc.tensor.transpose(BANKS[which][:, t * P:(t + 1) * P], src[:, t, :], ident[:, :])
                ins.then_inc(S[name], 1)

            def three(dst, ah, al, bh, bl, start=True, stop=True):
                nc.tensor.matmul(dst, ah, bh, start=start, stop=False)
                nc.tensor.matmul(dst, al, bh, start=False, stop=False)
                return nc.tensor.matmul(dst, ah, bl, start=False, stop=stop)

            def moe_up(n, j, slot):
                c = slice(j * P, (j + 1) * P)
                wait(pe, "gelu_done", n, j - 3)
                three(bank[j % 4][:, :], w1h[:, c], w1l[:, c], hh[slot][:, :], hl[slot][:, :]).then_inc(S["up_done"], 1)

            def moe_down(n, j):
                e, f = j // FT, j % FT
                c = slice(j * P, (j + 1) * P)
                pe.wait_ge(S["split_done"], at("split_done", n, j + 1))
                if f == 0:
                    wait(pe, "weighted_done", n, e - 1)
                three(bank[4 + e % 2][:, :], w2h[:, c], w2l[:, c], gh[j % RG], gl[j % RG],
                      start=f == 0, stop=f == FT - 1).then_inc(S["down_done"], 1)

            def moe(n, slot, beside):
                for j in range(3):
                    moe_up(n, j, slot)
                for j in range(J):
                    moe_down(n, j)
                    if j + 3 < J:
                        moe_up(n, j + 3, slot)
                    beside(j)

            def moe_back(s, n, nmoe):
                misc_free((f"z{s}_resid", n, 1))
                pe.wait_ge(S["summed"], at("summed", nmoe, E - 1))
                for t in range(T):
                    c = slice(t * P, (t + 1) * P)
                    nc.tensor.matmul(MISC[:, c], acc[:, c], ident[:, :], start=True, stop=False)
                    ins = nc.tensor.matmul(MISC[:, c], cwT[s - 1][:, c].bitcast(F32), b2[:, :], start=False, stop=True)
                ins.then_inc(S[f"z{s}_back"], 1)

            def router_1(r, slot, t_, n):
                misc_free((f"r{r}_pick", n, 1))
                for t in range(T):
                    c = slice(t * P, (t + 1) * P)
                    ins = three(MISC[:, t * E:(t + 1) * E], hh[slot][:, c], hl[slot][:, c], wrh[:, :], wrl[:, :])
                ins.then_inc(S[f"r{r}_logits"], 1)

            def router_2(r, n):
                misc_free((f"r{r}_cwT", n, 1))
                pe.wait_ge(S[f"r{r}_share"], at(f"r{r}_share", n, 9))
                for t in range(T):
                    ins = nc.tensor.transpose(MISC[0:2 * E, t * P:(t + 1) * P], cwp[:, t, :], ident[:, :])
                ins.then_inc(S[f"r{r}_turned"], 1)

            def spread_mix(r, n, e, which):
                name, k = mix_done(r, e)
                misc_free((name, n, k), which)
                pe.wait_ge(S[f"r{r}_cwT"], at(f"r{r}_cwT", n, 1))
                nc.tensor.matmul(BANKS[which][:, :], pick[:, e, :], cwT[r - 1][:, :], start=True, stop=True
                                 ).then_inc(S[f"r{r}_spread"], 1)

            def linear_1a(n, which):
                turn(nrm, lambda t: wait(pe, "lb_normed", n, t + 1), "xn_turned", n, ("xn_ready", n, 1), which)

            def linear_kv(n, c, which):
                misc_free(("kv_biased", n, c + 1), which)
                pe.wait_ge(S["xn_ready"], at("xn_ready", n, 1))
                for t in range(2):
                    ins = nc.tensor.matmul(BANKS[which][:, t * 2 * D:(t + 1) * 2 * D],
                                           xnT[:, (2 * c + t) * P:(2 * c + t + 1) * P], wqkv[:, D:3 * D],
                                           start=True, stop=True)
                ins.then_inc(S["kv_done"], 1)

            def linear_q(n, which):
                misc_free(("q_biased", n, 1), which)
                pe.wait_ge(S["xn_ready"], at("xn_ready", n, 1))
                nc.tensor.matmul(BANKS[which][:, :], wqkv[:, 0:D], xnT[:, :], start=True, stop=True
                                 ).then_inc(S["q_done"], 1)

            def linear_ktv(n, which):
                misc_free(("ktv_max", n, 1), which)
                pe.wait_ge(S["kv_biased"], at("kv_biased", n, 2))
                for t in range(T):
                    ins = nc.tensor.matmul(BANKS[which][:, 0:P], kv[:, t, 0:D], kv[:, t, D:2 * D],
                                           start=t == 0, stop=t == T - 1)
                ins.then_inc(S["ktv_done"], 1)

            def linear_2a(n):
                misc_free(("lin_copied", n, 1))
                pe.wait_ge(S["ktv_soft"], at("ktv_soft", n, 2))
                nc.tensor.matmul(MISC[:, :], sm[:, :], qT[:, :], start=True, stop=True).then_inc(S["lin_mixed"], 1)

            def linear_2b(n):
                misc_free(("x1_done", n, 1))
                for t in range(T):
                    c = slice(t * P, (t + 1) * P)
                    ins = nc.tensor.matmul(MISC[:, c], xnT[:, c], wout[:, :], start=True, stop=True)
                ins.then_inc(S["lin_out"], 1)

            pe.wait_ge(S["pool_const"], made["ident"])
            pe.wait_ge(S["ld_wqkv"], 16)
            pe.wait_ge(S["ld_wout"], 16)
            linear_1a(0, "PV")
            linear_kv(0, 0, "PV")
            linear_kv(0, 1, "MISC")
            linear_q(0, "PV")
            linear_ktv(0, "MISC")
            linear_2a(0)
            linear_2b(0)
            turn(h[0], lambda t: wait(pe, "l1_normed", 0, t + 1), "t1_turned", 0, ("t1_low", 0, 1))
            pe.wait_ge(S["dve_const"], made["pick_r"])
            router_1(1, 0, 1, 0)
            router_2(1, 0)
            spread_mix(1, 0, 0, "MISC")
            spread_mix(1, 0, 1, "PV")
            for k in ("b2a", "b2b", "wo"):
                pe.wait_ge(S["ld_" + k], 16)
            pe.wait_ge(S["w_low"], 8)

            def body(i, second, more):
                last = isinstance(i, int) and i == B
                n = i - 1
                if second:
                    read_by["MISC"] = ("o_normed", n, NG - 1)
                    read_by["PV"] = ("pv_copied", n, NG)

                def turn_3():
                    turn(h[1], lambda t: wait(pe, "l3_normed", n, t + 1), "t3_turned", n, ("t3_low", n, 1))

                def turn_2():
                    turn(nrm, lambda t: wait(pe, "l2_normed", i, t + 1), "t2_turned", i, ("t2_low", i, 1))

                def beside_1(j):
                    if j in (0, 4, 8, 12, 16, 20):
                        spread_mix(1, i, 2 + j // 4, "PV")
                    if not second:
                        if j == 10:
                            linear_1a(i + 1, "MISC")
                        if j in (14, 18):
                            linear_kv(i + 1, (j - 14) // 4, "MISC")
                        if j == 22:
                            linear_q(i + 1, "MISC")
                        if j == 26:
                            linear_ktv(i + 1, "MISC")
                        return
                    if j == 0:
                        values_back(n, NG - 1)
                    if j == 4:
                        o_turn(n)
                    if j == 8:
                        out_proj(n)
                    if j == 14:
                        turn_3()
                    if j == 19:
                        router_1(2, 1, 3, n)
                    if j == 25:
                        router_2(2, n)
                    if j == 29:
                        spread_mix(2, n, 0, "MISC")
                        spread_mix(2, n, 1, "PV")

                def beside_2(j):
                    if j == 1:
                        if not last:
                            moe_back(1, i, 2 * i - 1)
                        spread_mix(2, n, 2, "PV")
                    if j == 4:
                        spread_mix(2, n, 3, "PV")
                    if j in (5, 9, 17, 21):
                        spread_mix(2, n, {5: 4, 9: 5, 17: 6, 21: 7}[j], "MISC")
                    if last:
                        return
                    if j == 13:
                        turn_2()
                    if more:
                        if j == 8:
                            linear_1a(i + 1, "PV")
                        if j in (12, 16):
                            linear_kv(i + 1, (j - 12) // 4, "PV")
                        if j == 20:
                            linear_q(i + 1, "PV")
                        if j == 24:
                            linear_ktv(i + 1, "PV")

                if second:
                    pe.wait_ge(S["max_done"], at("max_done", n, 4 * NH))
                    pe.wait_ge(S["exp_done"], at("exp_done", n, 3 * NH))
                if not last:
                    moe(2 * i - 1 if second else 0, 0, beside_1)
                else:
                    values_back(n, NG - 1)
                    o_turn(n)
                    out_proj(n)
                    turn_3()
                    router_1(2, 1, 3, n)
                    router_2(2, n)
                    spread_mix(2, n, 0, "MISC")
                    spread_mix(2, n, 1, "PV")
                if second:
                    moe(2 * i - 1 if last else 2 * i, 1, beside_2)
                else:
                    moe_back(1, i, 0)
                    turn_2()
                if last:
                    moe_back(2, n, 2 * i - 1)
                    return
                nmoe = 2 * i if second else 0
                pe.wait_ge(S["gelu_done"], at("gelu_done", nmoe, J))
                for u in range(2 * NG):
                    g, s = u // 2, u % 2
                    c = slice(g * P, (g + 1) * P)
                    wait(pe, "stack_done", i, u - 5)
                    if u == 4:
                        pe.wait_ge(S["weighted_done"], at("weighted_done", nmoe, E))
                    if u == 0:
                        pe.wait_ge(S["t2_low"], at("t2_low", i, 1))
                        if not second:
                            pe.wait_ge(S["dve_const"], made["stacks"])
                    three(bank[u % 6][:, :], wsh[:, s, c], wsl[:, s, c], hh[0][:, :], hl[0][:, :]
                          ).then_inc(S["stack_mm"], 1)
                misc_free(("v_done", i, 1))
                for t in range(T):
                    c = slice(t * P, (t + 1) * P)
                    ins = three(MISC[:, c], hh[0][:, c], hl[0][:, c], wvh[:, :], wvl[:, :])
                ins.then_inc(S["v_mm"], 1)
                for s in range(NH + LAG):
                    if s == 0:
                        pe.wait_ge(S["stack_done"], at("stack_done", i, 2 * NG))
                    if s in (5, 9, 13, 17):
                        g = (s - 5) // 4
                        turn(spread, lambda t: wait(pe, "max_spread", i, 2 * g + 2) if t == 0 else None,
                             "max_turned", i, ("max_in_q", i, g + 1))
                    for u in range(3):
                        if s < NH:
                            g, rows = s // 4, slice((s % 4) * HS, (s % 4 + 1) * HS)
                            wait(pe, "max_done", i, 4 * (s - 1) + (1, 3, 4)[u])
                            for qt in ((3,), (2, 0), (1,))[u]:
                                c0 = Q_BANK[qt][1]
                                ins = nc.tensor.matmul(
                                    bank[u][:, c0:c0 + (qt + 1) * P], stack[g][1][rows, qt * P:(qt + 1) * P],
                                    stack[g][0][rows, 0:(qt + 1) * P], start=True, stop=True)
                            ins.then_inc(S["logit_mm"], 1)
                        if s >= LAG:
                            hd = s - LAG
                            g, rows = hd // 4, slice((hd % 4) * HS, (hd % 4 + 1) * HS)
                            pe.wait_ge(S["max_in_q"], at("max_in_q", i, g + 1))
                            wait(pe, "exp_done", i, 3 * (hd - 1) + u + 1)
                            for kt in ((0,), (1, 3), (2,))[u]:
                                b_, c0 = K_BANK[kt]
                                nc.tensor.matmul(
                                    bank[b_][:, c0:c0 + L - kt * P], stack[g][0][rows, kt * P:(kt + 1) * P],
                                    stack[g][1][rows, kt * P:L], start=True, stop=False)
                                ins = nc.tensor.matmul(bank[b_][:, c0:c0 + P], ident_b[:, :], later[:, :],
                                                       start=False, stop=True)
                            ins.then_inc(S["pair_mm"], 1)
                    if second and s == 0:
                        moe_back(2, i - 1, 2 * i)
                    if more:
                        if s == 1:
                            linear_2a(i + 1)
                        if s == 2:
                            linear_2b(i + 1)
                        if s == 6:
                            turn(h[0], lambda t: wait(pe, "l1_normed", i + 1, t + 1), "t1_turned", i + 1,
                                 ("t1_low", i + 1, 1))
                        if s == 8:
                            router_1(1, 0, 1, i + 1)
                        if s == 11:
                            router_2(1, i + 1)
                        if s == 14:
                            spread_mix(1, i + 1, 0, "MISC")
                        if s == 15:
                            spread_mix(1, i + 1, 1, "MISC")
                    if s in (12, 16, 20):
                        values_back(i, (s - 12) // 4)
                    if s in (10, 14, 18):
                        values(i, (s - 10) // 4)
                values(i, NG - 1)

            def o_turn(i):
                turn(o, lambda t: wait(pe, "o_normed", i, NG) if t == 0 else None, "o_turned", i, ("o_copied", i, 1))

            def out_proj(i):
                misc_free(("x3_done", i, 1))
                pe.wait_ge(S["o_copied"], at("o_copied", i, 1))
                for t in range(T):
                    c = slice(t * P, (t + 1) * P)
                    ins = nc.tensor.matmul(MISC[:, c], oT[:, c], wo[:, :], start=True, stop=True)
                ins.then_inc(S["wo_done"], 1)

            def values(i, g):
                pe.wait_ge(S["v_done"], at("v_done", i, 1))
                misc_free(("pv_copied", i, g + 1), "PV")
                pe.wait_ge(S["exp_done"], at("exp_done", i, 3 * (4 * g + 4)))
                for kt in range(T):
                    for j in range(4):
                        hd = 4 * g + j
                        a = (hd % RP) * PW + K_OFF[kt]
                        ins = nc.tensor.matmul(PV[j * HS:(j + 1) * HS, kt * P:L], V[:, kt, hd, :],
                                               work[:, a:a + L - kt * P], start=kt == 0, stop=kt == T - 1,
                                               skip_group_check=True)
                ins.then_inc(S["pv_done"], 1)

            def values_back(i, g):
                misc_free(("o_normed", i, g + 1))
                pe.wait_ge(S["pv_copied"], at("pv_copied", i, g + 1))
                for t in range(T):
                    ins = nc.tensor.transpose(MISC[:, t * P:(t + 1) * P], oT[:, t * P:(t + 1) * P], ident[:, :])
                ins.then_inc(S["pv_turned"], 1)

            every_iteration(pe, body)


def kernel(**a):
    import numpy as np
    import concourse.bacc as bacc
    from concourse.bass_utils import run_bass_kernel_spmd

    def f(name):
        return np.asarray(a[name])

    def c(v):
        return np.ascontiguousarray(v)

    w1, w2 = f("L0_ffn_W1"), f("L0_ffn_W2")
    laid = {
        "x": c(f("L0_attn_a_x")),
        "wqkv": c(f("L0_attn_a_w_qkv")),
        "bqkv": c(f("L0_attn_a_b_qkv")),
        "wout": c(f("L0_attn_a_w_out")),
        "bout": c(f("L0_attn_a_b_out")),
        "g": c(f("L0_attn_a_ln_g").reshape(P, 1)),
        "b": c(f("L0_attn_a_ln_b").reshape(P, 1)),
        "wq": c(f("L0_attn_b_Wq").T),
        "wk": c(f("L0_attn_b_Wk").T),
        "wv": c(f("L0_attn_b_Wv").T),
        "wo": c(f("L0_attn_b_Wo").T),
        "wr": c(f("L0_ffn_Wr").T),
        "br": c(f("L0_ffn_br")),
        "w1": c(w1.reshape(E * F, D).T),
        "b1": c(f("L0_ffn_b1").reshape(J, P).T),
        "w2": c(w2.reshape(E, D, FT, P).transpose(3, 0, 2, 1).reshape(P, J * D)),
        "b2": c(f("L0_ffn_b2")),
        "lnw": c(f("L0_ffn_ln_w")),
        "lnb": c(f("L0_ffn_ln_b")),
    }
    nc = bacc.Bacc("TRN2", target_bir_lowering=False, num_devices=1)
    w = {k: nc.dram_tensor(f"in_{k}", v.shape, mybir.dt.from_np(v.dtype), kind="ExternalInput").ap()
         for k, v in laid.items()}
    out = nc.dram_tensor("out", (B, L, D), F32, kind="ExternalOutput").ap()
    build(nc, w["x"], out, w)
    r = run_bass_kernel_spmd(nc, [{f"in_{k}": v for k, v in laid.items()}], core_ids=[0])
    return r.results[0]["out"]
```

```python
from contextlib import ExitStack

import concourse.bass as bass
import concourse.mybir as mybir
from concourse.alu_op_type import AluOpType as ALU

F32 = mybir.dt.float32
F32R = mybir.dt.float32r
BF16 = mybir.dt.bfloat16
U32 = mybir.dt.uint32
ACT = mybir.ActivationFunctionType
AX = mybir.AxisListType

P = 128
B, L, D = 8, 512, 128
T = L // P
NH, HD = 16, 8
HS = 32
NG = NH // 4
E, F = 8, 512
FT = F // P
J = E * FT
RG = 3
RP = 5
STACKS = [(0, 0), (0, 1), (1, 0), (1, 1), (2, 1), (3, 1), (2, 0), (3, 0)]
K_BY_ACT = [0, 1, 2, 3, 8, 9, 10, 11, 12, 13, 14, 15]
K_BY_POOL = [4, 5, 6, 7]
PW = 1280
LAG = 6
NEG = -3.0e38
SCALE = float(HD) ** -0.5
K_OFF = [0, 512, 1024, 896]
K_BANK = [(3, 0), (4, 0), (5, 0), (4, 384)]
Q_BANK = [(1, 384), (2, 0), (1, 0), (0, 0)]

BY_ACT = {1: [0], 2: [0, 2, 5, 6]}
BY_DVE = {1: [1, 2, 3, 4, 5, 6, 7], 2: [1, 3, 4, 7]}

PER = {}


def at(name, n, k):
    return PER[name] * n + k


def k_done(hd):
    for name, heads in (("act", K_BY_ACT), ("pool", K_BY_POOL)):
        if hd in heads:
            return f"k_placed_{name}", heads.index(hd) + 1


def mix_done(r, e):
    for name, experts in (("act", BY_ACT[r]), ("dve", BY_DVE[r])):
        if e in experts:
            return f"r{r}_mix_{name}", experts.index(e) + 1


def build(nc, x, out, w):
    ctx = ExitStack()
    with ctx:
        def sb(name, shape, dt=F32):
            return ctx.enter_context(nc.sbuf_tensor(name, shape, dt))

        S = {}

        def sem(name, per):
            S[name] = ctx.enter_context(nc.semaphore(name))
            PER[name] = per

        def wait(eng, name, n, k):
            v = at(name, n, k)
            if not isinstance(v, int) or v > 0:
                eng.wait_ge(S[name], v)

        def settle(eng):
            eng.nop(nofuse=True)

        ident = sb("ident", [P, P])
        head_mask = sb("head_mask", [P, P])
        ident_b = sb("ident_b", [P, P], BF16)
        later = sb("later", [P, P], BF16)
        expert_id = sb("expert_id", [P, T, 2, E])
        minus_half = sb("minus_half", [P, T])
        base_e = sb("base_e", [P, T])
        low_rows = sb("low_rows", [P, 2])
        max_rows = sb("max_rows", [P, 2])
        head_rows = sb("head_rows", [P, 4])
        pick = sb("pick", [2 * E, E, P], F32R)
        w1h, w1l = sb("w1h", [P, J * P], F32R), sb("w1l", [P, J * P], F32R)
        w2h, w2l = sb("w2h", [P, J * P], F32R), sb("w2l", [P, J * P], F32R)
        b1 = sb("b1", [P, J])
        b2 = sb("b2", [2 * E, D])
        wsh, wsl = sb("wsh", [P, 2, NG * P], F32R), sb("wsl", [P, 2, NG * P], F32R)
        wvh, wvl = sb("wvh", [P, D], F32R), sb("wvl", [P, D], F32R)
        wo = sb("wo", [P, D])
        wqkv = sb("wqkv", [P, 3 * D])
        wout = sb("wout", [P, D])
        wr_parts = sb("wr_parts", [P, 2, E], F32R)
        bkv = sb("bkv", [P, 2 * D])
        bout = sb("bout", [P, D])
        lnw, lnb = sb("lnw", [P, D]), sb("lnb", [P, D])
        br = sb("br", [P, E])
        cols = sb("cols", [P, 3])

        x0, xa, nrm = sb("x0", [P, T, D]), sb("xa", [P, T, D]), sb("nrm", [P, T, D])
        x1, x2, x3 = sb("x1", [P, T, D]), sb("x2", [P, T, D]), sb("x3", [P, T, D])
        h = [sb("h1", [P, T, D]), sb("h3", [P, T, D])]
        z = sb("z", [P, T, D])
        hh = [sb("hh0", [P, L], F32R), sb("hh1", [P, L], F32R)]
        hl = [sb("hl0", [P, L], F32R), sb("hl1", [P, L], F32R)]
        xnT = sb("xnT", [P, L])
        qT = sb("qT", [P, L])
        kv = sb("kv", [P, T, 2 * D])
        sm = sb("sm", [P, P])
        smx = sb("smx", [P, 4])
        cwT = [sb("cwT0", [2 * E, L], F32R), sb("cwT1", [2 * E, L], F32R)]
        mix = sb("mix", [P, E, L])
        acc = sb("acc", [P, L])
        work = sb("work", [P, 3 * PW])
        g32 = [work[:, PW + k * L:PW + (k + 1) * L] for k in range(RG)]
        weighted = [work[:, k * L:(k + 1) * L] for k in range(2)]
        parts = sb("parts", [P, 2 * RG * L], F32R)
        gh = [parts[:, k * L:(k + 1) * L] for k in range(RG)]
        gl = [parts[:, (RG + k) * L:(RG + k + 1) * L] for k in range(RG)]
        q_stack = [parts[:, g * L:(g + 1) * L] for g in range(NG)]
        stack_low = [parts[:, (NG + k) * L:(NG + k + 1) * L] for k in range(2)]
        k_stack = sb("k_stack", [P, 2, L], F32R)
        k_alone = [sb(f"k_alone{b}", [P, L], F32R) for b in range(8)]
        mix_flat = mix[:, :, :].rearrange("p e n -> p (e n)")

        def probs(hd, lo, hi):
            k = hd % RP
            if k < 3:
                return work[:, k * PW + lo:k * PW + hi]
            return mix_flat[:, 2 * L + (k - 3) * PW + lo:2 * L + (k - 3) * PW + hi]

        V = sb("V", [P, T, NH, HS])
        hmax = sb("hmax", [P, NG, 4, T])
        spread = sb("spread", [P, T, P])
        oT = sb("oT", [P, L])
        inv = sb("inv", [P, T, 4])
        o = sb("o", [P, T, D])
        LNS = ["la", "lb", "l1", "l2", "l3", "z1", "z2"]
        ln = {k: (sb(f"{k}_st", [P, T, 6]), sb(f"{k}_mv", [P, T, 2]), sb(f"{k}_ve", [P, T]), sb(f"{k}_rs", [P, T]))
              for k in LNS}
        lg = sb("lg", [P, T, E])
        top = sb("top", [P, T, E])
        topi = sb("topi", [P, T, E], U32)
        topf = sb("topf", [P, T, 2])
        gap, ratio, one_more = sb("gap", [P, T]), sb("ratio", [P, T]), sb("one_more", [P, T])
        share = sb("share", [P, T, 2])
        chosen = sb("chosen", [P, T, 2, E])
        cw = sb("cw", [P, T, E])
        cwp = sb("cwp", [P, T, 2 * E])

        bank = [ctx.enter_context(nc.psum_tensor(f"bank{k}", [P, L], F32)) for k in range(8)]
        PV, MISC = bank[6], bank[7]

        LOADS = ["w1", "w2", "w2b", "b1", "b2a", "b2b", "wk", "wq", "wv", "wo", "wqkv", "wout", "wr", "bkv", "bout",
                 "lnw", "br", "g", "b", "bq"]
        for k in LOADS:
            sem("ld_" + k, 16)
        sem("x_loaded", 16)
        sem("z_stored", 16)
        sem("pool_const", 1)
        sem("dve_const", 1)
        sem("w_high", 8)
        sem("w_low", 8)
        for k in LNS:
            sem(k + "_stats", T)
            sem(k + "_moments", T)
            sem(k + "_vareps", 1)
            sem(k + "_rstd", 1)
            sem(k + "_normed", T)
        sem("up_done", J)
        sem("gelu_done", J)
        sem("split_done", J)
        sem("down_done", J)
        sem("weighted_done", E)
        sem("summed", E - 1)
        for s in "12":
            sem(f"z{s}_back", 1)
            sem(f"z{s}_resid", 1)
            sem(f"z{s}_affine", 2)
            sem(f"x{2 * int(s) - 1}_biased", 1)
        for t in "123":
            sem(f"t{t}_turned", 1)
            sem(f"t{t}_high", 1)
            sem(f"t{t}_low", 1)
        for r in "12":
            sem(f"r{r}_logits", 1)
            sem(f"r{r}_pick", 11)
            sem(f"r{r}_ratio", 1)
            sem(f"r{r}_share", 9)
            sem(f"r{r}_turned", 1)
            sem(f"r{r}_cwT", 1)
            sem(f"r{r}_spread", E)
            sem(f"r{r}_mix_act", len(BY_ACT[int(r)]))
            sem(f"r{r}_mix_dve", len(BY_DVE[int(r)]))
        sem("x0_sums", 2)
        sem("xn_turned", 1)
        sem("xn_ready", 1)
        sem("kv_done", 2)
        sem("kv_biased", 2)
        sem("q_done", 1)
        sem("q_biased", 1)
        sem("ktv_done", 1)
        sem("ktv_max", 2)
        sem("ktv_exp", 1)
        sem("ktv_soft", 2)
        sem("lin_mixed", 1)
        sem("lin_copied", 1)
        sem("lin_out", 1)
        sem("x1_done", 1)
        sem("k_placed_act", len(K_BY_ACT))
        sem("k_placed_pool", len(K_BY_POOL))
        sem("stack_mm", 2 * NG)
        sem("stack_low", 2 * NG)
        sem("stack_done", 2 * NG)
        sem("v_mm", 1)
        sem("v_done", 1)
        sem("logit_mm", 3 * NH)
        sem("max_done", 4 * NH)
        sem("max_spread", 2 * NG)
        sem("max_turned", NG)
        sem("max_in_q", NG)
        sem("pair_mm", 3 * NH)
        sem("exp_done", 3 * NH)
        sem("pv_done", NG)
        sem("pv_copied", NG)
        sem("pv_turned", NG)
        sem("inv_done", NG)
        sem("o_normed", NG)
        sem("o_turned", 1)
        sem("o_copied", 1)
        sem("wo_done", 1)
        sem("x3_done", 1)

        x_tiles = x.rearrange("b (t p) d -> b p t d", p=P)
        out_tiles = out.rearrange("b (t p) d -> b p t d", p=P)

        def every_iteration(eng, body):
            body(0, False, True)
            with eng.Fori(1, B - 1) as i:
                body(i, True, True)
            body(B - 1, True, False)
            body(B, True, False)

        made = {}
        W_PARTS = []
        for k in range(4):
            c = slice(k * J * P // 4, (k + 1) * J * P // 4)
            W_PARTS.append((mix_flat[:, c], w1h[:, c], w1l[:, c]))
        w2_place = ((work[:, 0:1024], 0), (work[:, 1024:2048], 1024), (work[:, 2048:3584], 2048), (acc[:, :], 3584))
        for src, a in w2_place:
            c = slice(a, a + src.shape[-1])
            W_PARTS.append((src, w2h[:, c], w2l[:, c]))

        block = ctx.enter_context(nc.Block())

        @block.sync
        def _(sp):
            def load(name, dst, src):
                sp.dma_start(dst, src).then_inc(S["ld_" + name], 16)

            sp.dma_start(x0[:, :, :], x_tiles[0]).then_inc(S["x_loaded"], 16)
            load("wqkv", wqkv[:, :], w["wqkv"])
            load("g", cols[:, 0:1], w["g"])
            load("b", cols[:, 1:2], w["b"])
            load("bq", cols[:, 2:3], w["bqkv"][0:D].rearrange("(p a) -> p a", a=1))
            load("bkv", bkv[:, :], w["bqkv"][D:3 * D].partition_broadcast(P))
            load("bout", bout[:, :], w["bout"].partition_broadcast(P))
            load("wout", wout[:, :], w["wout"])
            load("wr", lg[:, 0, :], w["wr"])
            load("br", br[:, :], w["br"].partition_broadcast(P))
            sp.dma_start(lnb[:, :], w["lnb"].partition_broadcast(P)).then_inc(S["z_stored"], 16)
            load("w1", mix[:, :, :], w["w1"].rearrange("p (e n) -> p e n", e=E))
            load("w2", work[:, 0:J * P - L], w["w2"][:, 0:J * P - L])
            load("w2b", acc[:, :], w["w2"][:, J * P - L:J * P])
            load("b1", b1[:, :], w["b1"])
            load("b2a", b2[0:E, :], w["b2"])
            load("b2b", b2[E:2 * E, :], w["b2"])
            load("wk", x2[:, 0, :], w["wk"])
            load("wq", x2[:, 1, :], w["wq"])
            load("wv", x2[:, 2, :], w["wv"])
            load("wo", wo[:, :], w["wo"])
            load("lnw", lnw[:, :], w["lnw"].partition_broadcast(P))

            def body(i, second, more):
                if more:
                    sp.wait_ge(S["x1_done"], at("x1_done", i, 1))
                    sp.dma_start(x0[:, :, :], x_tiles[i + 1]).then_inc(S["x_loaded"], 16)
                if second:
                    sp.wait_ge(S["z2_affine"], at("z2_affine", i - 1, 2))
                    sp.dma_start(out_tiles[i - 1], z[:, :, :]).then_inc(S["z_stored"], 16)

            every_iteration(sp, body)
            sp.wait_ge(S["z_stored"], at("z_stored", B, 16))

        @block.gpsimd
        def _(gp):
            consts = [0]

            def const(ins):
                ins.then_inc(S["pool_const"], 1)
                consts[0] += 1
                gp.wait_ge(S["pool_const"], consts[0])

            def keep(ap, op, fill, base, pattern, mult):
                const(nc.gpsimd.affine_select(out=ap, in_=ap, compare_op=op, fill=fill, base=base,
                                              pattern=pattern, channel_multiplier=mult))

            def rstd(k, n, eps):
                st, mv, ve, rs = ln[k]
                gp.wait_ge(S[k + "_moments"], at(k + "_moments", n, T))
                settle(gp)
                nc.gpsimd.tensor_scalar(ve[:, :], mv[:, :, 1], eps, None, ALU.add).then_inc(S[k + "_vareps"], 1)
                gp.wait_ge(S[k + "_vareps"], at(k + "_vareps", n, 1))
                nc.gpsimd.tensor_tensor(rs[:, :], ve[:, :], minus_half[:, :], ALU.pow).then_inc(S[k + "_rstd"], 1)

            def router(r, n):
                gp.wait_ge(S[f"r{r}_pick"], at(f"r{r}_pick", n, 11))
                nc.gpsimd.tensor_tensor(ratio[:, :], base_e[:, :], gap[:, :], ALU.pow).then_inc(S[f"r{r}_ratio"], 1)

            def moe_sum(n, e):
                gp.wait_ge(S["weighted_done"], at("weighted_done", n, e + 1))
                if e > 1:
                    gp.wait_ge(S["summed"], at("summed", n, e - 1))
                nc.gpsimd.tensor_tensor(acc[:, :], acc[:, :], weighted[e % 2], ALU.add).then_inc(S["summed"], 1)

            def bias_x(s, xt, n):
                k = ("l1", "l3")[s]
                gp.wait_ge(S[k + "_normed"], at(k + "_normed", n, T))
                nc.gpsimd.tensor_tensor(xt[:, :, :], xt[:, :, :], lnb[:, None, :].to_broadcast([P, T, D]),
                                        ALU.add).then_inc(S[f"x{2 * s + 1}_biased"], 1)

            def affine(s, n, xin, dst):
                gp.wait_ge(S[f"z{s}_normed"], at(f"z{s}_normed", n, T))
                nc.gpsimd.tensor_tensor(z[:, :, :], z[:, :, :], lnw[:, None, :].to_broadcast([P, T, D]),
                                        ALU.mult).then_inc(S[f"z{s}_affine"], 1)
                gp.wait_ge(S[f"z{s}_affine"], at(f"z{s}_affine", n, 1))
                gp.wait_ge(S[f"x{2 * s - 1}_biased"], at(f"x{2 * s - 1}_biased", n, 1))
                nc.gpsimd.tensor_tensor(dst[:, :, :], z[:, :, :], xin[:, :, :], ALU.add).then_inc(S[f"z{s}_affine"], 1)

            def place_k(i, hd):
                g = hd // 4
                gp.wait_ge(S["stack_done"], at("stack_done", i, STACKS.index((g, 0)) + 1))
                settle(gp)
                nc.gpsimd.tensor_scalar(k_alone[hd % 8][:, :], k_stack[:, g % 2, :].bitcast(F32),
                                        head_rows[:, hd % 4:hd % 4 + 1], None, ALU.mult).then_inc(S["k_placed_pool"], 1)

            def x0_plus_xa(n):
                gp.wait_ge(S["la_normed"], at("la_normed", n, T))
                nc.gpsimd.tensor_tensor(x0[:, :, :], x0[:, :, :], xa[:, :, :], ALU.add).then_inc(S["x0_sums"], 1)

            def x0_plus_bias(n):
                gp.wait_ge(S["x0_sums"], at("x0_sums", n, 1))
                nc.gpsimd.tensor_tensor(x0[:, :, :], x0[:, :, :], bout[:, None, :].to_broadcast([P, T, D]),
                                        ALU.add).then_inc(S["x0_sums"], 1)

            const(nc.gpsimd.memset(minus_half[:, :], -0.5))
            const(nc.gpsimd.memset(base_e[:, :], 2.718281828459045))
            const(nc.gpsimd.memset(ident[:, :], 0.0))
            keep(ident[:, :], ALU.not_equal, 1.0, 0, [[-1, P]], 1)
            made["ident"] = consts[0]
            rstd("la", 0, 1e-5)
            gp.wait_ge(S["ld_bout"], 16)
            x0_plus_xa(0)
            rstd("lb", 0, 1e-5)
            x0_plus_bias(0)
            const(nc.gpsimd.memset(head_mask[:, :], 0.0))
            hm = head_mask[:, :].rearrange("p (h e) -> p h e", e=HD)
            keep(hm, ALU.is_ge, NEG, 0, [[-HD, NH], [0, HD]], 1)
            keep(hm, ALU.is_ge, NEG, HD - 1, [[HD, NH], [0, HD]], -1)
            made["head_mask"] = consts[0]
            for half in range(2):
                pv = (x3, o)[half][0:2 * E, :, :]
                const(nc.gpsimd.memset(pv, 0.0))
                for r in range(2):
                    keep(pv, ALU.not_equal, 1.0, -(half * E // 2 + r * E), [[-1, E // 2], [0, P]], 1)
            made["pick"] = consts[0]
            const(nc.gpsimd.iota(expert_id[:, :, :, :], [[0, T], [0, 2], [1, E]], base=0, channel_multiplier=0,
                                 allow_small_or_imprecise_dtypes=True))
            made["expert_id"] = consts[0]
            rstd("l1", 0, 1e-5)
            gp.wait_ge(S["z_stored"], at("z_stored", 0, 16))
            bias_x(0, x1, 0)
            router(1, 0)
            const(nc.gpsimd.memset(ident_b[:, :], 0.0))
            keep(ident_b[:, :], ALU.not_equal, 1.0, 0, [[-1, P]], 1)
            const(nc.gpsimd.memset(later[:, :], 0.0))
            keep(later[:, :], ALU.is_ge, NEG, 0, [[1, P]], -1)
            const(nc.gpsimd.memset(head_rows[:, :], 1.0))
            keep(head_rows[:, :], ALU.is_ge, 0.0, 0, [[-HS, 4]], 1)
            keep(head_rows[:, :], ALU.is_ge, 0.0, HS - 1, [[HS, 4]], -1)
            const(nc.gpsimd.memset(h[1][:, :, :], 0.0))
            for k, (lo, hi) in enumerate(((HD, 2 * HD), (2 * HD, 3 * HD), (3 * HD, 3 * HD + 2))):
                const(nc.gpsimd.memset(h[1][:, k, :].rearrange("p (j r) -> p j r", r=HS)[:, :, lo:hi], 1.0))
            const(nc.gpsimd.memset(V[:, :, :, :], 0.0))
            const(nc.gpsimd.memset(V[:, :, :, HD:HD + 1], 1.0))
            const(nc.gpsimd.memset(spread[:, :, :], 0.0))
            made["all"] = consts[0]
            gp.wait_ge(S["ld_lnw"], 16)

            def body(i, second, more):
                last = isinstance(i, int) and i == B
                if last:
                    rstd("l3", i - 1, 1e-5)
                    bias_x(1, x3, i - 1)
                    router(2, i - 1)
                else:
                    for e in range(1, E):
                        if second:
                            if e == 2:
                                rstd("l3", i - 1, 1e-5)
                            if e == 3:
                                bias_x(1, x3, i - 1)
                            if e == 5:
                                router(2, i - 1)
                            if e == 6 and more:
                                rstd("la", i + 1, 1e-5)
                            if e == 7 and more:
                                x0_plus_xa(i + 1)
                        elif e == 1:
                            rstd("la", i + 1, 1e-5)
                            x0_plus_xa(i + 1)
                            rstd("lb", i + 1, 1e-5)
                            x0_plus_bias(i + 1)
                        moe_sum(2 * i - 1 if second else 0, e)
                if second:
                    for e in range(1, E):
                        if not last:
                            if e == 1:
                                if more:
                                    rstd("lb", i + 1, 1e-5)
                                    x0_plus_bias(i + 1)
                                rstd("z1", i, 1e-12)
                                affine(1, i, x1, x2)
                                rstd("l2", i, 1e-5)
                        moe_sum(2 * i - 1 if last else 2 * i, e)
                else:
                    rstd("z1", i, 1e-12)
                    affine(1, i, x1, x2)
                    rstd("l2", i, 1e-5)
                if last:
                    rstd("z2", i - 1, 1e-12)
                    affine(2, i - 1, x3, z)
                    return
                for hd in K_BY_POOL:
                    place_k(i, hd)
                if more:
                    rstd("l1", i + 1, 1e-5)
                    bias_x(0, x1, i + 1)
                if second:
                    rstd("z2", i - 1, 1e-12)
                if more:
                    router(1, i + 1)
                if second:
                    affine(2, i - 1, x3, z)

            every_iteration(gp, body)

        @block.scalar
        def _(ac):
            def act(out_, in_, fn, name, **kw):
                return nc.scalar.activation(out_, in_, fn, **kw).then_inc(S[name], 1)

            def high_part(t, slot, n):
                ac.wait_ge(S[f"t{t}_turned"], at(f"t{t}_turned", n, 1))
                act(hh[slot][:, :], MISC[:, :], ACT.Copy, f"t{t}_high")

            def router(r, n):
                ac.wait_ge(S[f"r{r}_turned"], at(f"r{r}_turned", n, 1))
                act(cwT[r - 1][:, :], MISC[0:2 * E, :], ACT.Copy, f"r{r}_cwT")

            def mix_copy(r, n, e, src, nmoe=None):
                assert mix_done(r, e)[0] == f"r{r}_mix_act"
                ac.wait_ge(S[f"r{r}_spread"], at(f"r{r}_spread", n, e + 1))
                if nmoe is not None:
                    ac.wait_ge(S["weighted_done"], at("weighted_done", nmoe, e + 1))
                act(mix[:, e, :], src[:, :], ACT.Copy, f"r{r}_mix_act")

            def moe_gelu(n, j):
                ac.wait_ge(S["up_done"], at("up_done", n, j + 1))
                wait(ac, "split_done", n, j - RG + 1)
                nc.scalar.activation(g32[j % RG], bank[j % 4][:, :], ACT.Gelu, bias=b1[:, j:j + 1])
                wait(ac, "down_done", n, j - RG + 1)
                act(gh[j % RG], bank[j % 4][:, :], ACT.Gelu, "gelu_done", bias=b1[:, j:j + 1])

            def moe(n, beside):
                for j in range(J):
                    moe_gelu(n, j)
                    beside(j)

            def linear_1a(n, src):
                ac.wait_ge(S["xn_turned"], at("xn_turned", n, 1))
                act(xnT[:, :], src[:, :], ACT.Identity, "xn_ready", scale=cols[:, 0:1], bias=cols[:, 1:2])

            def linear_1b(n, src):
                ac.wait_ge(S["q_done"], at("q_done", n, 1))
                act(qT[:, :], src[:, :], ACT.Identity, "q_biased", bias=cols[:, 2:3])

            def linear_2a(n):
                ac.wait_ge(S["ktv_max"], at("ktv_max", n, 2))
                act(sm[:, :], sm[:, :], ACT.Exp, "ktv_exp", bias=smx[:, 0:1], accum_out=smx[:, 1:2])

            def linear_2b(n):
                ac.wait_ge(S["lin_mixed"], at("lin_mixed", n, 1))
                act(xnT[:, :], MISC[:, :], ACT.Copy, "lin_copied")

            def pv_copy(i, g):
                ac.wait_ge(S["pv_done"], at("pv_done", i, g + 1))
                wait(ac, "pv_turned", i, g)
                act(oT[:, :], PV[:, :], ACT.Copy, "pv_copied")

            def o_copy(i):
                ac.wait_ge(S["o_turned"], at("o_turned", i, 1))
                act(oT[:, :], MISC[:, :], ACT.Copy, "o_copied")

            for k in ("g", "b", "bq"):
                ac.wait_ge(S["ld_" + k], 16)

            def weight_high(k):
                if k == 0:
                    ac.wait_ge(S["ld_w1"], 16)
                if k == 4:
                    ac.wait_ge(S["ld_w2"], 16)
                    ac.wait_ge(S["ld_w2b"], 16)
                src, hi, _ = W_PARTS[k]
                act(hi, src, ACT.Copy, "w_high")

            linear_1a(0, PV)
            weight_high(0)
            weight_high(1)
            linear_1b(0, PV)
            weight_high(2)
            weight_high(3)
            linear_2a(0)
            weight_high(4)
            linear_2b(0)
            weight_high(5)
            weight_high(6)
            weight_high(7)
            high_part(1, 0, 0)
            router(1, 0)
            ac.wait_ge(S["w_low"], 4)
            mix_copy(1, 0, 0, MISC)
            ac.wait_ge(S["ld_b1"], 16)
            ac.wait_ge(S["w_low"], 8)

            def body(i, second, more):
                last = isinstance(i, int) and i == B

                def beside_1(j):
                    if not second:
                        if j == 13:
                            linear_1a(i + 1, MISC)
                        if j == 25:
                            linear_1b(i + 1, MISC)
                        return
                    if j == 1:
                        pv_copy(i - 1, NG - 1)
                    if j == 7:
                        o_copy(i - 1)
                    if j == 17:
                        high_part(3, 1, i - 1)
                    if j == 28:
                        router(2, i - 1)

                def beside_2(j):
                    n1 = None if last else 2 * i - 1
                    if j == 0 and not last:
                        mix_copy(2, i - 1, 0, MISC, n1)
                    if j == 4:
                        mix_copy(2, i - 1, 2, PV, n1)
                    if j == 12:
                        mix_copy(2, i - 1, 5, MISC, n1)
                    if j == 16 and not last:
                        high_part(2, 0, i)
                    if j == 20:
                        mix_copy(2, i - 1, 6, MISC, n1)
                    if more:
                        if j == 11:
                            linear_1a(i + 1, PV)
                        if j == 23:
                            linear_1b(i + 1, PV)

                if not last:
                    moe(2 * i - 1 if second else 0, beside_1)
                else:
                    pv_copy(i - 1, NG - 1)
                    o_copy(i - 1)
                    high_part(3, 1, i - 1)
                    router(2, i - 1)
                    mix_copy(2, i - 1, 0, MISC)
                if second:
                    moe(2 * i - 1 if last else 2 * i, beside_2)
                    if last:
                        return
                else:
                    high_part(2, 0, i)
                if more:
                    linear_2a(i + 1)
                def low_stack(u, src):
                    ac.wait_ge(S["stack_mm"], at("stack_mm", i, u + 1))
                    wait(ac, "stack_done", i, u - 1)
                    s = STACKS[u][1]
                    act(stack_low[u % 2], src[:, :], ACT.Copy, "stack_low", scale=low_rows[:, s:s + 1])

                def place_k(hd):
                    g = hd // 4
                    ac.wait_ge(S["stack_done"], at("stack_done", i, STACKS.index((g, 0)) + 1))
                    if hd >= 8:
                        ac.wait_ge(S["pair_mm"], at("pair_mm", i, 3 * (hd - 7)))
                    act(k_alone[hd % 8][:, :], k_stack[:, g % 2, :].bitcast(F32), ACT.Copy, "k_placed_act",
                        scale=head_rows[:, hd % 4:hd % 4 + 1])

                low_stack(0, bank[0])
                low_stack(1, bank[1])
                place_k(0)
                low_stack(2, bank[2])
                place_k(1)
                low_stack(3, bank[3])
                place_k(2)
                place_k(3)
                ac.wait_ge(S["v_mm"], at("v_mm", i, 1))
                act(V[:, :, :, 0:HD], MISC[:, :].rearrange("p (t h d) -> p t h d", t=T, d=HD), ACT.Copy, "v_done")
                low_stack(4, bank[4])
                low_stack(5, bank[5])
                for s in range(NH + LAG):
                    if 8 <= s + 1 < NH:
                        place_k(s + 1)
                    if s >= LAG:
                        hd = s - LAG
                        if hd >= RP:
                            ac.wait_ge(S["pv_done"], at("pv_done", i, (hd - RP) // 4 + 1))
                        for u, (lo, hi) in enumerate(((0, 512), (512, 1024), (1024, 1280))):
                            ac.wait_ge(S["pair_mm"], at("pair_mm", i, 3 * hd + u + 1))
                            act(probs(hd, lo, hi), bank[3 + u][:, 0:hi - lo], ACT.Exp, "exp_done", scale=SCALE)
                    if s in (1, 5):
                        low_stack(6 + s // 5, PV)
                    if more:
                        if s == 1:
                            linear_2b(i + 1)
                        if s == 6:
                            high_part(1, 0, i + 1)
                        if s == 15:
                            router(1, i + 1)
                        if s == 18:
                            mix_copy(1, i + 1, 0, MISC)
                    if s >= LAG + 5 and (s - LAG - 5) % 4 == 0:
                        pv_copy(i, (s - LAG - 5) // 4)
                nc.scalar.activation(smx[:, 3:4], cols[:, 2:3], ACT.Gelu)

            every_iteration(ac, body)

        @block.vector
        def _(ve):
            def stats(k, src, n):
                st, mv, _, _ = ln[k]
                for t in range(T):
                    nc.vector.bn_stats(st[:, t, :], src[:, t, :]).then_inc(S[k + "_stats"], 1)
                ve.wait_ge(S[k + "_stats"], at(k + "_stats", n, T))
                settle(ve)
                for t in range(T):
                    nc.vector.bn_aggr(mv[:, t, :], st[:, t, :]).then_inc(S[k + "_moments"], 1)

            def norm(k, dst, src, n):
                st, mv, _, rs = ln[k]
                ve.wait_ge(S[k + "_rstd"], at(k + "_rstd", n, 1))
                for t in range(T):
                    nc.vector.tensor_scalar(dst[:, t, :], src[:, t, :], mv[:, t, 0:1], rs[:, t:t + 1],
                                            ALU.subtract, ALU.mult).then_inc(S[k + "_normed"], 1)

            consts = [0]

            def const(ins):
                ins.then_inc(S["dve_const"], 1)
                consts[0] += 1

            def settled():
                ve.wait_ge(S["dve_const"], consts[0])

            def split(hi, lo, src):
                const(nc.vector.tensor_copy(hi, src))
                settled()
                const(nc.vector.tensor_tensor(lo, src, hi.bitcast(F32), ALU.subtract))

            def weight_low(k):
                src, hi, lo = W_PARTS[k]
                ve.wait_ge(S["w_high"], k + 1)
                nc.vector.tensor_tensor(lo, src, hi.bitcast(F32), ALU.subtract).then_inc(S["w_low"], 1)

            def low_part(t, slot, n):
                ve.wait_ge(S[f"t{t}_high"], at(f"t{t}_high", n, 1))
                nc.vector.tensor_tensor(hl[slot][:, :], MISC[:, :], hh[slot][:, :].bitcast(F32),
                                        ALU.subtract).then_inc(S[f"t{t}_low"], 1)

            def router_1(r, n):
                k = f"r{r}_pick"
                ve.wait_ge(S[f"r{r}_logits"], at(f"r{r}_logits", n, 1))
                both = MISC[:, 0:T * 2 * E].rearrange("p (t s e) -> p t s e", s=2, e=E)
                nc.vector.tensor_tensor(lg[:, :, :], both[:, :, 0, :], br[:, None, :].to_broadcast([P, T, E]),
                                        ALU.add).then_inc(S[k], 1)
                ve.wait_ge(S[k], at(k, n, 1))
                nc.vector.tensor_tensor(lg[:, :, :], lg[:, :, :], both[:, :, 1, :], ALU.add).then_inc(S[k], 1)
                ve.wait_ge(S[k], at(k, n, 2))
                settle(ve)
                for t in range(T):
                    nc.vector.max(top[:, t, :], lg[:, t, :]).then_inc(S[k], 1)
                ve.wait_ge(S[k], at(k, n, 6))
                nc.vector.tensor_tensor(gap[:, :], top[:, :, 1], top[:, :, 0], ALU.subtract).then_inc(S[k], 1)
                for t in range(T):
                    nc.vector.max_index(topi[:, t, :], top[:, t, :], lg[:, t, :]).then_inc(S[k], 1)

            def router_2(r, n):
                k = f"r{r}_share"
                ve.wait_ge(S[f"r{r}_pick"], at(f"r{r}_pick", n, 11))
                nc.vector.tensor_copy(topf[:, :, :], topi[:, :, 0:2]).then_inc(S[k], 1)
                ve.wait_ge(S[f"r{r}_ratio"], at(f"r{r}_ratio", n, 1))
                nc.vector.tensor_scalar(one_more[:, :], ratio[:, :], 1.0, None, ALU.add).then_inc(S[k], 1)
                ve.wait_ge(S[k], at(k, n, 2))
                nc.vector.reciprocal(share[:, :, 0], one_more[:, :]).then_inc(S[k], 1)
                nc.vector.tensor_tensor(chosen[:, :, :, :], expert_id[:, :, :, :],
                                        topf[:, :, :, None].to_broadcast([P, T, 2, E]),
                                        ALU.is_equal).then_inc(S[k], 1)
                ve.wait_ge(S[k], at(k, n, 4))
                nc.vector.tensor_tensor(share[:, :, 1], share[:, :, 0], ratio[:, :], ALU.mult).then_inc(S[k], 1)
                ve.wait_ge(S[k], at(k, n, 5))
                nc.vector.tensor_tensor(chosen[:, :, :, :], chosen[:, :, :, :],
                                        share[:, :, :, None].to_broadcast([P, T, 2, E]),
                                        ALU.mult).then_inc(S[k], 1)
                ve.wait_ge(S[k], at(k, n, 6))
                nc.vector.tensor_tensor(cw[:, :, :], chosen[:, :, 0, :], chosen[:, :, 1, :], ALU.add).then_inc(S[k], 1)
                ve.wait_ge(S[k], at(k, n, 7))
                nc.vector.tensor_copy(cwp[:, :, 0:E].bitcast(F32R), cw[:, :, :]).then_inc(S[k], 1)
                ve.wait_ge(S[k], at(k, n, 8))
                nc.vector.tensor_tensor(cwp[:, :, E:2 * E], cw[:, :, :], cwp[:, :, 0:E], ALU.subtract).then_inc(S[k], 1)

            def moe_split(n, j):
                ve.wait_ge(S["gelu_done"], at("gelu_done", n, j + 1))
                wait(ve, "down_done", n, j - RG + 1)
                nc.vector.tensor_tensor(gl[j % RG], g32[j % RG], gh[j % RG].bitcast(F32),
                                        ALU.subtract).then_inc(S["split_done"], 1)

            def mix_copy(r, n, e, src, nmoe=None):
                assert mix_done(r, e)[0] == f"r{r}_mix_dve"
                ve.wait_ge(S[f"r{r}_spread"], at(f"r{r}_spread", n, e + 1))
                if nmoe is not None:
                    ve.wait_ge(S["weighted_done"], at("weighted_done", nmoe, e + 1))
                nc.vector.tensor_copy(mix[:, e, :], src[:, :]).then_inc(S[f"r{r}_mix_dve"], 1)

            def moe_weigh(n, e, r, nb, acc_read):
                name, k = mix_done(r, e)
                ve.wait_ge(S["down_done"], at("down_done", n, FT * e + FT))
                ve.wait_ge(S[name], at(name, nb, k))
                if e == 0 and acc_read is not None:
                    wait(ve, *acc_read)
                if e >= 2:
                    wait(ve, "summed", n, e - 2)
                nc.vector.tensor_tensor(acc[:, :] if e == 0 else weighted[e % 2], bank[4 + e % 2][:, :],
                                        mix[:, e, :], ALU.mult).then_inc(S["weighted_done"], 1)

            def moe(n, r, nb, beside, acc_read=None):
                for j in range(J):
                    moe_split(n, j)
                    if j >= 5 and (j - 5) % FT == 0:
                        moe_weigh(n, (j - 5) // FT, r, nb, acc_read)
                    beside(j)
                moe_weigh(n, E - 1, r, nb, None)

            def end_moe(s, n, z_free):
                ve.wait_ge(S[f"z{s}_back"], at(f"z{s}_back", n, 1))
                wait(ve, *z_free)
                nc.vector.tensor_tensor(z[:, :, :], MISC[:, :].rearrange("p (t d) -> p t d", t=T), h[s - 1][:, :, :],
                                        ALU.add).then_inc(S[f"z{s}_resid"], 1)

            def z_stats(s, n):
                ve.wait_ge(S[f"z{s}_resid"], at(f"z{s}_resid", n, 1))
                stats(f"z{s}", z, n)

            def linear_a(n):
                ve.wait_ge(S["x_loaded"], at("x_loaded", n, 16))
                stats("la", x0, n)

            def linear_b(n):
                ve.wait_ge(S["la_normed"], at("la_normed", n, T))
                stats("lb", xa, n)

            def linear_kv(n, c, src):
                ve.wait_ge(S["kv_done"], at("kv_done", n, c + 1))
                nc.vector.tensor_tensor(kv[:, 2 * c:2 * c + 2, :], src[:, :].rearrange("p (t d) -> p t d", t=2),
                                        bkv[:, None, :].to_broadcast([P, 2, 2 * D]), ALU.add).then_inc(S["kv_biased"], 1)

            def linear_max(n, src):
                ve.wait_ge(S["ktv_done"], at("ktv_done", n, 1))
                nc.vector.tensor_tensor(sm[:, :], src[:, 0:P], head_mask[:, :], ALU.add).then_inc(S["ktv_max"], 1)
                ve.wait_ge(S["ktv_max"], at("ktv_max", n, 1))
                nc.vector.tensor_reduce(smx[:, 0:1], sm[:, :], AX.X, ALU.max, negate=True).then_inc(S["ktv_max"], 1)

            def linear_2a(n):
                ve.wait_ge(S["ktv_exp"], at("ktv_exp", n, 1))
                nc.vector.reciprocal(smx[:, 2:3], smx[:, 1:2]).then_inc(S["ktv_soft"], 1)
                ve.wait_ge(S["ktv_soft"], at("ktv_soft", n, 1))
                nc.vector.tensor_scalar(sm[:, :], sm[:, :], smx[:, 2:3], None, ALU.mult).then_inc(S["ktv_soft"], 1)

            def linear_2b(n):
                ve.wait_ge(S["lin_out"], at("lin_out", n, 1))
                ve.wait_ge(S["x0_sums"], at("x0_sums", n, 2))
                nc.vector.tensor_tensor(x1[:, :, :], MISC[:, :].rearrange("p (t d) -> p t d", t=T), x0[:, :, :],
                                        ALU.add).then_inc(S["x1_done"], 1)

            linear_a(0)
            norm("la", xa, x0, 0)
            for k in ("bkv", "wr", "br"):
                ve.wait_ge(S["ld_" + k], 16)
            split(wr_parts[:, 0, :], wr_parts[:, 1, :], lg[:, 0, :])
            settled()
            made["wr"] = consts[0]
            linear_b(0)
            norm("lb", nrm, xa, 0)
            linear_kv(0, 0, PV)
            linear_kv(0, 1, MISC)
            weight_low(0)
            ve.wait_ge(S["pool_const"], made["head_mask"])
            linear_max(0, MISC)
            weight_low(1)
            linear_2a(0)
            weight_low(2)
            weight_low(3)
            linear_2b(0)
            ve.wait_ge(S["x1_done"], at("x1_done", 0, 1))
            stats("l1", x1, 0)
            weight_low(4)
            norm("l1", h[0], x1, 0)
            ve.wait_ge(S["pool_const"], made["pick"])
            for half in range(2):
                const(nc.vector.tensor_copy(pick[:, half * E // 2:(half + 1) * E // 2, :], (x3, o)[half][0:2 * E, :, :]))
            made["pick_r"] = consts[0]
            low_part(1, 0, 0)
            router_1(1, 0)
            weight_low(5)
            weight_low(6)
            ve.wait_ge(S["pool_const"], made["expert_id"])
            router_2(1, 0)
            weight_low(7)
            ve.wait_ge(S["w_low"], 4)
            mix_copy(1, 0, 1, PV)

            def row_masks():
                ve.wait_ge(S["pool_const"], made["all"])
                const(nc.vector.memset(max_rows[:, :], 0.0))
                const(nc.vector.tensor_tensor(z[:, 0:3, :], h[1][:, 0:3, :],
                                              ident[:, None, :].to_broadcast([P, 3, P]), ALU.mult))
                settled()
                const(nc.vector.tensor_reduce(low_rows[:, :], z[:, 0:2, :], AX.X, ALU.add))
                const(nc.vector.tensor_reduce(max_rows[:, 0:1], z[:, 2, :], AX.X, ALU.add))

            def stack_weights(s):
                for k in ("wk", "wq", "wv"):
                    ve.wait_ge(S["ld_" + k], 16)
                dst = x3[:, :, :].rearrange("p t (g r) -> p (t g) r", r=HS)
                src = x2[:, s, :].rearrange("p (h d) -> p h d", d=HD)
                settled()
                const(nc.vector.memset(x3[:, :, :], 0.0))
                settled()
                for r in range(3):
                    const(nc.vector.tensor_copy(dst[:, :, r * HD:(r + 1) * HD], src))
                settled()
                split(wsh[:, s, :], wsl[:, s, :], x3[:, :, :].rearrange("p t n -> p (t n)"))

            def body(i, second, more):
                last = isinstance(i, int) and i == B

                def beside_1(j):
                    if j in (3, 7, 11, 15, 19, 23):
                        mix_copy(1, i, 2 + j // 4, PV)
                    if second and more:
                        if j == 28:
                            linear_a(i + 1)
                        if j == 30:
                            norm("la", xa, x0, i + 1)
                    if not second:
                        if j == 2:
                            linear_a(i + 1)
                        if j == 4:
                            norm("la", xa, x0, i + 1)
                        if j == 6:
                            linear_b(i + 1)
                        if j == 8:
                            norm("lb", nrm, xa, i + 1)
                        if j in (17, 21):
                            linear_kv(i + 1, (j - 17) // 4, MISC)
                        if j == 29:
                            linear_max(i + 1, MISC)
                        if j == 24:
                            row_masks()
                        if j in (26, 28):
                            stack_weights((j - 26) // 2)
                        if j == 30:
                            split(wvh[:, :], wvl[:, :], x2[:, 2, :])
                            settled()
                            made["stacks"] = consts[0]
                        return
                    if j == 3:
                        normalize(i - 1, NG - 1)
                    if j == 11:
                        x3_sum(i - 1, ("summed", 2 * i - 1, 1))
                    if j == 13:
                        norm("l3", h[1], x3, i - 1)
                    if j == 18:
                        low_part(3, 1, i - 1)
                    if j == 22:
                        router_1(2, i - 1)
                    if j == 24:
                        router_2(2, i - 1)

                def beside_2(j):
                    n1 = None if last else 2 * i - 1
                    if j == 0 and not last:
                        mix_copy(2, i - 1, 1, PV, n1)
                    if j == 7:
                        mix_copy(2, i - 1, 3, PV, n1)
                    if j == 8:
                        mix_copy(2, i - 1, 4, MISC, n1)
                    if j == 24:
                        mix_copy(2, i - 1, 7, MISC, n1)
                    if last:
                        return
                    if j == 4:
                        end_moe(1, i, ("z_stored", i, 0))
                        z_stats(1, i)
                    if j == 6:
                        norm("z1", z, z, i)
                    if j == 9:
                        ve.wait_ge(S["z1_affine"], at("z1_affine", i, 2))
                        stats("l2", x2, i)
                    if j == 11:
                        wait(ve, "xn_turned", i + 1 if more else i, 1)
                        norm("l2", nrm, x2, i)
                    if j == 17:
                        low_part(2, 0, i)
                    if more:
                        if j == 1:
                            linear_b(i + 1)
                        if j == 3:
                            ve.wait_ge(S["t2_turned"], at("t2_turned", i - 1, 1))
                            norm("lb", nrm, xa, i + 1)
                        if j in (15, 19):
                            linear_kv(i + 1, (j - 15) // 4, PV)
                        if j == 27:
                            linear_max(i + 1, PV)

                if not last:
                    moe(2 * i - 1 if second else 0, 1, i, beside_1)
                else:
                    normalize(i - 1, NG - 1)
                    x3_sum(i - 1, ("z2_affine", i - 2, 2))
                    norm("l3", h[1], x3, i - 1)
                    low_part(3, 1, i - 1)
                    router_1(2, i - 1)
                    router_2(2, i - 1)
                    mix_copy(2, i - 1, 1, PV)
                if second:
                    moe(2 * i - 1 if last else 2 * i, 2, i - 1, beside_2,
                        None if last else ("z1_back", i, 1))
                else:
                    end_moe(1, i, ("z_stored", i, 0))
                    z_stats(1, i)
                    norm("z1", z, z, i)
                    ve.wait_ge(S["z1_affine"], at("z1_affine", i, 2))
                    stats("l2", x2, i)
                    ve.wait_ge(S["xn_turned"], at("xn_turned", i + 1, 1))
                    norm("l2", nrm, x2, i)
                    low_part(2, 0, i)
                if last:
                    end_moe(2, i - 1, ("z_stored", i - 1, 16))
                    z_stats(2, i - 1)
                    norm("z2", z, z, i - 1)
                    return
                if more:
                    linear_2a(i + 1)
                def full_stack(u, src):
                    g, s = STACKS[u]
                    ve.wait_ge(S["stack_low"], at("stack_low", i, u + 1))
                    if s == 0 and g >= 2:
                        wait(ve, "k_placed_act" if g == 2 else "k_placed_pool", i, 4)
                    nc.vector.scalar_tensor_tensor(
                        out=(k_stack[:, g % 2, :], q_stack[g])[s], in0=src[:, :], scalar=max_rows[:, s:s + 1],
                        in1=stack_low[u % 2].bitcast(F32), op0=ALU.add, op1=ALU.subtract,
                    ).then_inc(S["stack_done"], 1)

                for u in range(3):
                    full_stack(u, bank[u])
                for s in range(NH + LAG):
                    if s in (5, 9, 13, 16):
                        g = (s - 4) // 4
                        ve.wait_ge(S["max_turned"], at("max_turned", i, g + 1))
                        nc.vector.tensor_tensor(q_stack[g], q_stack[g].bitcast(F32), MISC[:, :],
                                                ALU.subtract).then_inc(S["max_in_q"], 1)
                    if s < NH:
                        g, j = s // 4, s % 4
                        for k, qt in enumerate((3, 2, 0, 1)):
                            b_, c = Q_BANK[qt]
                            n_ = (qt + 1) * P
                            ve.wait_ge(S["logit_mm"], at("logit_mm", i, 3 * s + b_ + 1))
                            nc.vector.tensor_reduce(hmax[:, g, j, qt:qt + 1], bank[b_][:, c:c + n_], AX.X,
                                                    ALU.max).then_inc(S["max_done"], 1)
                        if j == 3:
                            src = hmax[:, g, :, :].rearrange("p j t -> p t j")
                            dst = spread[:, :, :].rearrange("p t (j r) -> p t j r", r=HS)
                            ve.wait_ge(S["max_done"], at("max_done", i, 4 * s + 4))
                            wait(ve, "max_turned", i, g)
                            nc.vector.tensor_copy(dst[:, :, :, 3 * HD].bitcast(F32R), src).then_inc(S["max_spread"], 1)
                            ve.wait_ge(S["max_spread"], at("max_spread", i, 2 * g + 1))
                            nc.vector.tensor_tensor(dst[:, :, :, 3 * HD + 1], src, dst[:, :, :, 3 * HD],
                                                    ALU.subtract).then_inc(S["max_spread"], 1)
                    if s < 3:
                        full_stack(3 + s, bank[3 + s])
                    if s in (3, 6):
                        full_stack(6 + s // 6, PV)
                    if second:
                        if s == 0:
                            end_moe(2, i - 1, ("z1_affine", i, 2))
                        if s == 8:
                            z_stats(2, i - 1)
                        if s == 10:
                            norm("z2", z, z, i - 1)
                    if more:
                        if s == 2:
                            linear_2b(i + 1)
                        if s == 4:
                            ve.wait_ge(S["x1_done"], at("x1_done", i + 1, 1))
                            stats("l1", x1, i + 1)
                        if s == 5:
                            norm("l1", h[0], x1, i + 1)
                        if s == 7:
                            low_part(1, 0, i + 1)
                        if s == 10:
                            router_1(1, i + 1)
                        if s == 14:
                            router_2(1, i + 1)
                        if s == 19:
                            mix_copy(1, i + 1, 1, MISC)
                    if s in (12, 17, 20):
                        normalize(i, (s - 12) // 4)

            def x3_sum(i, x3_free):
                ve.wait_ge(S["wo_done"], at("wo_done", i, 1))
                wait(ve, *x3_free)
                nc.vector.tensor_tensor(x3[:, :, :], MISC[:, :].rearrange("p (t d) -> p t d", t=T), x2[:, :, :],
                                        ALU.add).then_inc(S["x3_done"], 1)
                ve.wait_ge(S["x3_done"], at("x3_done", i, 1))
                stats("l3", x3, i)

            def normalize(i, g):
                ve.wait_ge(S["pv_turned"], at("pv_turned", i, g + 1))
                wait(ve, "o_normed", i, g)
                src = MISC[:, :].rearrange("p (t j r) -> p t j r", t=T, r=HS)
                nc.vector.reciprocal(inv[:, :, :], src[:, :, :, HD]).then_inc(S["inv_done"], 1)
                ve.wait_ge(S["inv_done"], at("inv_done", i, g + 1))
                nc.vector.tensor_tensor(
                    o[:, :, :].rearrange("p t (g j d) -> p t g j d", g=NG, d=HD)[:, :, g], src[:, :, :, 0:HD],
                    inv[:, :, :, None].to_broadcast([P, T, 4, HD]), ALU.mult).then_inc(S["o_normed"], 1)

            every_iteration(ve, body)

        @block.tensor
        def _(pe):
            BANKS = {"MISC": MISC, "PV": PV}
            read_by = {}

            def misc_free(reader, which="MISC"):
                if which in read_by:
                    wait(pe, *read_by[which])
                read_by[which] = reader

            def turn(src, name, n, reader, which="MISC"):
                misc_free(reader, which)
                for t in range(T):
                    ins = nc.tensor.transpose(BANKS[which][:, t * P:(t + 1) * P], src[:, t, :], ident[:, :])
                ins.then_inc(S[name], 1)

            def three(dst, ah, al, bh, bl, start=True, stop=True):
                nc.tensor.matmul(dst, ah, bh, start=start, stop=False)
                nc.tensor.matmul(dst, al, bh, start=False, stop=False)
                return nc.tensor.matmul(dst, ah, bl, start=False, stop=stop)

            def moe_up(n, j, slot):
                c = slice(j * P, (j + 1) * P)
                wait(pe, "gelu_done", n, j - 3)
                three(bank[j % 4][:, :], w1h[:, c], w1l[:, c], hh[slot][:, :], hl[slot][:, :]).then_inc(S["up_done"], 1)

            def moe_down(n, j):
                e, f = j // FT, j % FT
                c = slice(j * P, (j + 1) * P)
                pe.wait_ge(S["split_done"], at("split_done", n, j + 1))
                if f == 0:
                    wait(pe, "weighted_done", n, e - 1)
                three(bank[4 + e % 2][:, :], w2h[:, c], w2l[:, c], gh[j % RG], gl[j % RG],
                      start=f == 0, stop=f == FT - 1).then_inc(S["down_done"], 1)

            def moe(n, slot, beside, last_values_of=None):
                for j in range(3):
                    moe_up(n, j, slot)
                if last_values_of is not None:
                    values(last_values_of, NG - 1)
                for j in range(J):
                    moe_down(n, j)
                    if j + 3 < J:
                        moe_up(n, j + 3, slot)
                    beside(j)

            def moe_back(s, n, nmoe):
                misc_free((f"z{s}_resid", n, 1))
                pe.wait_ge(S["summed"], at("summed", nmoe, E - 1))
                for t in range(T):
                    c = slice(t * P, (t + 1) * P)
                    nc.tensor.matmul(MISC[:, c], acc[:, c], ident[:, :], start=True, stop=False)
                    ins = nc.tensor.matmul(MISC[:, c], cwT[s - 1][:, c].bitcast(F32), b2[:, :], start=False, stop=True)
                ins.then_inc(S[f"z{s}_back"], 1)

            def router_1(r, slot, n):
                misc_free((f"r{r}_pick", n, 2))
                for t in range(T):
                    c, o_ = slice(t * P, (t + 1) * P), 2 * E * t
                    nc.tensor.matmul(MISC[:, o_:o_ + 2 * E], hh[slot][:, c], wr_parts[:, :, :], start=True, stop=True)
                    ins = nc.tensor.matmul(MISC[:, o_:o_ + E], hl[slot][:, c], wr_parts[:, 0, :],
                                           start=False, stop=True, skip_group_check=True)
                ins.then_inc(S[f"r{r}_logits"], 1)

            def router_2(r, n):
                misc_free((f"r{r}_cwT", n, 1))
                pe.wait_ge(S[f"r{r}_share"], at(f"r{r}_share", n, 9))
                for t in range(T):
                    ins = nc.tensor.transpose(MISC[0:2 * E, t * P:(t + 1) * P], cwp[:, t, :], ident[:, :])
                ins.then_inc(S[f"r{r}_turned"], 1)

            def spread_mix(r, n, e, which):
                name, k = mix_done(r, e)
                misc_free((name, n, k), which)
                pe.wait_ge(S[f"r{r}_cwT"], at(f"r{r}_cwT", n, 1))
                nc.tensor.matmul(BANKS[which][:, :], pick[:, e, :], cwT[r - 1][:, :], start=True, stop=True
                                 ).then_inc(S[f"r{r}_spread"], 1)

            def linear_1a(n, which):
                pe.wait_ge(S["lb_normed"], at("lb_normed", n, T))
                turn(nrm, "xn_turned", n, ("xn_ready", n, 1), which)

            def linear_kv(n, c, which):
                misc_free(("kv_biased", n, c + 1), which)
                pe.wait_ge(S["xn_ready"], at("xn_ready", n, 1))
                for t in range(2):
                    ins = nc.tensor.matmul(BANKS[which][:, t * 2 * D:(t + 1) * 2 * D],
                                           xnT[:, (2 * c + t) * P:(2 * c + t + 1) * P], wqkv[:, D:3 * D],
                                           start=True, stop=True)
                ins.then_inc(S["kv_done"], 1)

            def linear_q(n, which):
                misc_free(("q_biased", n, 1), which)
                pe.wait_ge(S["xn_ready"], at("xn_ready", n, 1))
                nc.tensor.matmul(BANKS[which][:, :], wqkv[:, 0:D], xnT[:, :], start=True, stop=True
                                 ).then_inc(S["q_done"], 1)

            def linear_ktv(n, which):
                misc_free(("ktv_max", n, 1), which)
                pe.wait_ge(S["kv_biased"], at("kv_biased", n, 2))
                for t in range(T):
                    ins = nc.tensor.matmul(BANKS[which][:, 0:P], kv[:, t, 0:D], kv[:, t, D:2 * D],
                                           start=t == 0, stop=t == T - 1)
                ins.then_inc(S["ktv_done"], 1)

            def linear_2a(n):
                misc_free(("lin_copied", n, 1))
                pe.wait_ge(S["ktv_soft"], at("ktv_soft", n, 2))
                nc.tensor.matmul(MISC[:, :], sm[:, :], qT[:, :], start=True, stop=True).then_inc(S["lin_mixed"], 1)

            def linear_2b(n):
                misc_free(("x1_done", n, 1))
                for t in range(T):
                    c = slice(t * P, (t + 1) * P)
                    ins = nc.tensor.matmul(MISC[:, c], xnT[:, c], wout[:, :], start=True, stop=True)
                ins.then_inc(S["lin_out"], 1)

            pe.wait_ge(S["pool_const"], made["ident"])
            pe.wait_ge(S["ld_wqkv"], 16)
            pe.wait_ge(S["ld_wout"], 16)
            linear_1a(0, "PV")
            linear_kv(0, 0, "PV")
            linear_kv(0, 1, "MISC")
            linear_q(0, "PV")
            linear_ktv(0, "MISC")
            linear_2a(0)
            linear_2b(0)
            pe.wait_ge(S["l1_normed"], at("l1_normed", 0, T))
            turn(h[0], "t1_turned", 0, ("t1_low", 0, 1))
            pe.wait_ge(S["dve_const"], made["pick_r"])
            router_1(1, 0, 0)
            router_2(1, 0)
            spread_mix(1, 0, 0, "MISC")
            spread_mix(1, 0, 1, "PV")
            for k in ("b2a", "b2b", "wo"):
                pe.wait_ge(S["ld_" + k], 16)
            pe.wait_ge(S["w_low"], 8)

            def body(i, second, more):
                last = isinstance(i, int) and i == B
                n = i - 1
                if second:
                    read_by["MISC"] = ("o_normed", n, NG - 1)
                    read_by["PV"] = ("pv_copied", n, NG - 1)

                def turn_3():
                    pe.wait_ge(S["l3_normed"], at("l3_normed", n, T))
                    turn(h[1], "t3_turned", n, ("t3_low", n, 1))

                def turn_2():
                    pe.wait_ge(S["l2_normed"], at("l2_normed", i, T))
                    turn(nrm, "t2_turned", i, ("t2_low", i, 1))

                def beside_1(j):
                    if j in (0, 4, 8, 12, 16, 20):
                        spread_mix(1, i, 2 + j // 4, "PV")
                    if not second:
                        if j == 10:
                            linear_1a(i + 1, "MISC")
                        if j in (14, 18):
                            linear_kv(i + 1, (j - 14) // 4, "MISC")
                        if j == 22:
                            linear_q(i + 1, "MISC")
                        if j == 26:
                            linear_ktv(i + 1, "MISC")
                        return
                    if j == 0:
                        values_back(n, NG - 1)
                    if j == 4:
                        o_turn(n)
                    if j == 8:
                        out_proj(n)
                    if j == 14:
                        turn_3()
                    if j == 19:
                        router_1(2, 1, n)
                    if j == 25:
                        router_2(2, n)
                    if j == 29:
                        spread_mix(2, n, 0, "MISC")
                        spread_mix(2, n, 1, "PV")

                def beside_2(j):
                    if j == 1:
                        if not last:
                            moe_back(1, i, 2 * i - 1)
                        spread_mix(2, n, 2, "PV")
                    if j == 4:
                        spread_mix(2, n, 3, "PV")
                    if j in (5, 9, 17, 21):
                        spread_mix(2, n, {5: 4, 9: 5, 17: 6, 21: 7}[j], "MISC")
                    if last:
                        return
                    if j == 13:
                        turn_2()
                    if more:
                        if j == 8:
                            linear_1a(i + 1, "PV")
                        if j in (12, 16):
                            linear_kv(i + 1, (j - 12) // 4, "PV")
                        if j == 20:
                            linear_q(i + 1, "PV")
                        if j == 24:
                            linear_ktv(i + 1, "PV")

                if second:
                    pe.wait_ge(S["max_done"], at("max_done", n, 4 * NH))
                if not last:
                    moe(2 * i - 1 if second else 0, 0, beside_1, n if second else None)
                else:
                    values(n, NG - 1)
                    values_back(n, NG - 1)
                    o_turn(n)
                    out_proj(n)
                    turn_3()
                    router_1(2, 1, n)
                    router_2(2, n)
                    spread_mix(2, n, 0, "MISC")
                    spread_mix(2, n, 1, "PV")
                if second:
                    moe(2 * i - 1 if last else 2 * i, 1, beside_2)
                else:
                    moe_back(1, i, 0)
                    turn_2()
                if last:
                    moe_back(2, n, 2 * i - 1)
                    return
                nmoe = 2 * i if second else 0
                pe.wait_ge(S["gelu_done"], at("gelu_done", nmoe, J))
                for u, (g, s) in enumerate(STACKS[:6]):
                    c = slice(g * P, (g + 1) * P)
                    if u == 4:
                        pe.wait_ge(S["weighted_done"], at("weighted_done", nmoe, E))
                    if u == 0:
                        pe.wait_ge(S["t2_low"], at("t2_low", i, 1))
                        if not second:
                            pe.wait_ge(S["dve_const"], made["stacks"])
                    three(bank[u][:, :], wsh[:, s, c], wsl[:, s, c], hh[0][:, :], hl[0][:, :]
                          ).then_inc(S["stack_mm"], 1)
                misc_free(("v_done", i, 1))
                for t in range(T):
                    c = slice(t * P, (t + 1) * P)
                    ins = three(MISC[:, c], hh[0][:, c], hl[0][:, c], wvh[:, :], wvl[:, :])
                ins.then_inc(S["v_mm"], 1)
                for s in range(NH + LAG):
                    if s == 0:
                        pe.wait_ge(S["stack_done"], at("stack_done", i, 3))
                    if s == LAG:
                        pe.wait_ge(S["stack_done"], at("stack_done", i, 6))
                    if s in (5, 9, 13):
                        turn_maxima(i, (s - 5) // 4)
                    for u in range(3):
                        if s < NH:
                            g = s // 4
                            if u == 0:
                                name, k = k_done(s)
                                pe.wait_ge(S[name], at(name, i, k))
                            wait(pe, "max_done", i, 4 * (s - 1) + (1, 3, 4)[u])
                            for qt in ((3,), (2, 0), (1,))[u]:
                                c0 = Q_BANK[qt][1]
                                nc.tensor.matmul(
                                    bank[u][:, c0:c0 + (qt + 1) * P], q_stack[g][:, qt * P:(qt + 1) * P],
                                    k_alone[s % 8][:, 0:(qt + 1) * P], start=True, stop=False)
                                ins = nc.tensor.matmul(bank[u][:, c0 + qt * P:c0 + (qt + 1) * P], later[:, :],
                                                       ident_b[:, :], start=False, stop=True)
                            ins.then_inc(S["logit_mm"], 1)
                        if s >= LAG:
                            hd = s - LAG
                            g = hd // 4
                            pe.wait_ge(S["max_in_q"], at("max_in_q", i, g + 1))
                            wait(pe, "exp_done", i, 3 * (hd - 1) + u + 1)
                            for kt in ((0,), (1, 3), (2,))[u]:
                                b_, c0 = K_BANK[kt]
                                nc.tensor.matmul(
                                    bank[b_][:, c0:c0 + L - kt * P], k_alone[hd % 8][:, kt * P:(kt + 1) * P],
                                    q_stack[g][:, kt * P:L], start=True, stop=False)
                                ins = nc.tensor.matmul(bank[b_][:, c0:c0 + P], ident_b[:, :], later[:, :],
                                                       start=False, stop=True)
                            ins.then_inc(S["pair_mm"], 1)
                    if s == 16:
                        turn_maxima(i, 3)
                    if second and s == 0:
                        moe_back(2, i - 1, 2 * i)
                    if s in (0, 4):
                        u = 6 + s // 4
                        g, k = STACKS[u]
                        c = slice(g * P, (g + 1) * P)
                        misc_free(("stack_done", i, u + 1), "PV")
                        three(PV[:, :], wsh[:, k, c], wsl[:, k, c], hh[0][:, :], hl[0][:, :]).then_inc(S["stack_mm"], 1)
                    if more:
                        if s == 1:
                            linear_2a(i + 1)
                        if s == 2:
                            linear_2b(i + 1)
                        if s == 6:
                            pe.wait_ge(S["l1_normed"], at("l1_normed", i + 1, T))
                            turn(h[0], "t1_turned", i + 1,
                                 ("t1_low", i + 1, 1))
                        if s == 10:
                            router_1(1, 0, i + 1)
                        if s == 15:
                            router_2(1, i + 1)
                        if s == 18:
                            spread_mix(1, i + 1, 0, "MISC")
                        if s == 19:
                            spread_mix(1, i + 1, 1, "MISC")
                    if s in (12, 17, 20):
                        values_back(i, (s - 12) // 4)
                    if s in (10, 14, 18):
                        values(i, (s - 10) // 4)

            def o_turn(i):
                pe.wait_ge(S["o_normed"], at("o_normed", i, NG))
                turn(o, "o_turned", i, ("o_copied", i, 1))

            def out_proj(i):
                misc_free(("x3_done", i, 1))
                pe.wait_ge(S["o_copied"], at("o_copied", i, 1))
                for t in range(T):
                    c = slice(t * P, (t + 1) * P)
                    ins = nc.tensor.matmul(MISC[:, c], oT[:, c], wo[:, :], start=True, stop=True)
                ins.then_inc(S["wo_done"], 1)

            def turn_maxima(i, g):
                pe.wait_ge(S["max_spread"], at("max_spread", i, 2 * g + 2))
                turn(spread, "max_turned", i, ("max_in_q", i, g + 1))

            def values(i, g):
                pe.wait_ge(S["v_done"], at("v_done", i, 1))
                misc_free(("pv_copied", i, g + 1), "PV")
                pe.wait_ge(S["exp_done"], at("exp_done", i, 3 * (4 * g + 4)))
                for kt in range(T):
                    for j in range(4):
                        hd = 4 * g + j
                        a = K_OFF[kt]
                        ins = nc.tensor.matmul(PV[j * HS:(j + 1) * HS, kt * P:L], V[:, kt, hd, :],
                                               probs(hd, a, a + L - kt * P), start=kt == 0, stop=kt == T - 1,
                                               skip_group_check=True)
                ins.then_inc(S["pv_done"], 1)

            def values_back(i, g):
                misc_free(("o_normed", i, g + 1))
                pe.wait_ge(S["pv_copied"], at("pv_copied", i, g + 1))
                for t in range(T):
                    ins = nc.tensor.transpose(MISC[:, t * P:(t + 1) * P], oT[:, t * P:(t + 1) * P], ident[:, :])
                ins.then_inc(S["pv_turned"], 1)

            every_iteration(pe, body)


def kernel(**a):
    import numpy as np
    import concourse.bacc as bacc
    from concourse.bass_utils import run_bass_kernel_spmd

    def f(name):
        return np.asarray(a[name])

    def c(v):
        return np.ascontiguousarray(v)

    w1, w2 = f("L0_ffn_W1"), f("L0_ffn_W2")
    laid = {
        "x": c(f("L0_attn_a_x")),
        "wqkv": c(f("L0_attn_a_w_qkv")),
        "bqkv": c(f("L0_attn_a_b_qkv")),
        "wout": c(f("L0_attn_a_w_out")),
        "bout": c(f("L0_attn_a_b_out")),
        "g": c(f("L0_attn_a_ln_g").reshape(P, 1)),
        "b": c(f("L0_attn_a_ln_b").reshape(P, 1)),
        "wq": c(f("L0_attn_b_Wq").T),
        "wk": c(f("L0_attn_b_Wk").T),
        "wv": c(f("L0_attn_b_Wv").T),
        "wo": c(f("L0_attn_b_Wo").T),
        "wr": c(f("L0_ffn_Wr").T),
        "br": c(f("L0_ffn_br")),
        "w1": c(w1.reshape(E * F, D).T),
        "b1": c(f("L0_ffn_b1").reshape(J, P).T),
        "w2": c(w2.reshape(E, D, FT, P).transpose(3, 0, 2, 1).reshape(P, J * D)),
        "b2": c(f("L0_ffn_b2")),
        "lnw": c(f("L0_ffn_ln_w")),
        "lnb": c(f("L0_ffn_ln_b")),
    }
    nc = bacc.Bacc("TRN2", target_bir_lowering=False, num_devices=1)
    w = {k: nc.dram_tensor(f"in_{k}", v.shape, mybir.dt.from_np(v.dtype), kind="ExternalInput").ap()
         for k, v in laid.items()}
    out = nc.dram_tensor("out", (B, L, D), F32, kind="ExternalOutput").ap()
    build(nc, w["x"], out, w)
    r = run_bass_kernel_spmd(nc, [{f"in_{k}": v for k, v in laid.items()}], core_ids=[0])
    return r.results[0]["out"]
```
